# Optimizing a Trainium2 kernel written in Bass

```python
import numpy as np
import jax
import jax.numpy as jnp

def _softmax(x, axis=-1):
    return jax.nn.softmax(x, axis=axis)

def _gelu(x):
    return jax.nn.gelu(x, approximate=True)

def _silu(x):
    return jax.nn.silu(x)

def _sigmoid(x):
    return jax.nn.sigmoid(x)

def _layernorm(x, axis=-1, eps=1e-05):
    m = jnp.mean(x, axis=axis, keepdims=True)
    v = jnp.var(x, axis=axis, keepdims=True)
    return (x - m) / jnp.sqrt(v + eps)

def _scatter_add(tgt, idx, src, axis=0):
    return tgt.at[idx].add(src)

def _segment_sum(src, seg, n):
    return jax.ops.segment_sum(src, seg, n)
kernel_name = 'mk_gnn_preln_d1_gnn_r64_054b67'

def setup_inputs(seed: int=0):
    np.random.seed(seed)
    _w = jnp.asarray

    def _rec_inputs():
        import jax
        import jax.numpy as jnp
        _gk = jax.random.key(seed)
        x = -0.0005207 + 1.001 * jax.random.normal(jax.random.fold_in(_gk, 1), (100000, 128), jnp.float32)
        src = jax.random.randint(jax.random.fold_in(_gk, 2), (25000,), 0, 100000, jnp.int32)
        dst = jnp.minimum((100000 * jax.random.uniform(jax.random.fold_in(_gk, 3), (25000,)) ** 2.0).astype(jnp.int32), 99999)
        _o = jnp.argsort(dst, stable=True)
        src = src[_o]
        dst = dst[_o]
        edge_type_50 = jax.random.randint(jax.random.fold_in(_gk, 12), (25000,), 0, 50, jnp.int32)
        return (x, src, dst, edge_type_50)
    x, src, dst, edge_type_50 = _rec_inputs()

    def _L0_gnn_setup():
        import jax, jax.numpy as jnp
        import numpy as np
        N_ENT = 256
        N_REL = 50
        D = 128
        B = 4
        E = 4096
        key = jax.random.key(seed)
        k1, k2, k3, k4, k5, k6 = jax.random.split(key, 6)
        x = jax.random.normal(k1, (N_ENT, D), dtype=jnp.float32)
        bases = jax.random.normal(k2, (B, D, D), dtype=jnp.float32) * 0.05
        comps = jax.random.normal(k3, (N_REL, B), dtype=jnp.float32)
        alpha = jax.random.normal(k4, (N_REL, 1), dtype=jnp.float32)
        edge_index = jax.random.randint(k5, (2, E), 0, N_ENT, dtype=jnp.int64)
        edge_type = jax.random.randint(k6, (E,), 0, N_REL, dtype=jnp.int64)
        return {'x': x, 'bases': bases, 'comps': comps, 'alpha': alpha, 'edge_index': edge_index, 'edge_type': edge_type}
    _L0_gnn_all = _L0_gnn_setup()
    _L0_gnn_in = {k: v for k, v in _L0_gnn_all.items() if k in ('bases', 'comps', 'alpha')}
    del _L0_gnn_all
    return {'x': x, 'src': src, 'dst': dst, 'edge_type_50': edge_type_50, 'L0_gnn_bases': _L0_gnn_in['bases'], 'L0_gnn_comps': _L0_gnn_in['comps'], 'L0_gnn_alpha': _L0_gnn_in['alpha']}

def reference(x, src, dst, edge_type_50, L0_gnn_bases, L0_gnn_comps, L0_gnn_alpha):
    import jax
    import jax.numpy as jnp

    def _L0_gnn_ref(x, bases, comps, alpha, edge_index, edge_type):
        import jax, jax.numpy as jnp
        import numpy as np
        N_ENT = 256
        N_REL = 50
        D = 128
        B = 4
        E = 4096
        n = x.shape[0]
        row, col = (edge_index[0], edge_index[1])
        ones = jnp.ones(row.shape, x.dtype)
        deg = jax.ops.segment_sum(ones, row, num_segments=n)
        deg_inv = jnp.where(deg > 0, jax.lax.rsqrt(jnp.maximum(deg, 1.0)), 0.0)
        norm = deg_inv[row] * deg_inv[col]
        h_j = x[col]
        c_e = comps[edge_type]
        hj_b = c_e[:, :, None] * h_j[:, None, :]
        msg = jnp.einsum('ebd,bdf->ef', hj_b, bases)
        msg = msg * alpha[edge_type] * norm[:, None]
        out = jax.ops.segment_sum(msg, row, num_segments=n)
        return out
    edge_index = jnp.stack([src, dst])
    h = jnp.maximum(_layernorm(x, axis=-1), 0.0)
    x = x + _L0_gnn_ref(h, L0_gnn_bases, L0_gnn_comps, L0_gnn_alpha, edge_index, edge_type_50)
    return x

_drawn_inputs = setup_inputs


def setup_inputs(seed=0):
    import zlib

    import numpy as np

    out = dict(_drawn_inputs(seed))
    spreads = {}
    factors = {}
    for name, (base, spread) in spreads.items():
        noise = np.random.default_rng([zlib.crc32(name.encode()), seed]).standard_normal(out[name].shape)
        drawn = base * np.exp(spread * noise) if base else spread * noise
        out[name] = jnp.asarray(drawn.astype(out[name].dtype))
    for name, factor in factors.items():
        out[name] = (out[name] * factor).astype(out[name].dtype)
    return out
```

```python
from contextlib import ExitStack

import concourse.bass as bass
from concourse import mybir

ALU = mybir.AluOpType
ACT = mybir.ActivationFunctionType
F32 = mybir.dt.float32
F16 = mybir.dt.float16
BF16 = mybir.dt.bfloat16
I32 = mybir.dt.int32

P = 128
GROUP = 4
EPS = 1e-5


def padded_rows(nodes):
    return -(-(nodes + GROUP * P + 1) // P) * P


def build(nc, x, src, dst, edge_type, bases, comps, alpha, out):
    N, D = x.shape
    E = src.shape[0]
    R, B = comps.shape
    TILES = -(-E // P)
    GROUPS = TILES // GROUP
    HALF = TILES // 2
    assert D == P and TILES == GROUPS * GROUP and TILES == 2 * HALF and HALF <= P and GROUPS % 2 == 1
    LAST_ROWS = E // P - HALF
    LAST_EDGES = E % P
    LAST_GROUP = E - (GROUPS - 1) * GROUP * P
    SPARE = N
    PAD_NODE = N + GROUP * P
    CHUNKS = 7
    CH = -(-(PAD_NODE // P + 1) // CHUNKS)
    CH += CH % 2
    HI = CHUNKS * CH
    BANK = 512
    PARTS = 2
    LOW = 2048
    SPLITS = 3
    COPIES = 2 * (GROUPS + 1)
    COPY_ROWS = N // COPIES
    EARLY_COPIES = COPIES - (GROUPS - 3)
    ROOT_AT, STORE_AT = 34, 40
    INVERT_AT = 16
    LEAD = 26
    W = GROUP * P
    assert COPY_ROWS * COPIES == N and E < PARTS * LOW * LOW

    inverse_root_dram = nc.dram_tensor("inverse_root_table", (HI * P, 1), F32, kind="Internal").ap()
    edge_row_dram = nc.dram_tensor("edge_rows", (2, TILES * P), F16, kind="Internal").ap()

    with ExitStack() as ctx:
        def sb(name, shape, dt=F32):
            return ctx.enter_context(nc.sbuf_tensor(name, shape, dt))

        def sem(name):
            return ctx.enter_context(nc.semaphore(name))

        table_i = sb("table_i", [HALF, 6, P], I32)
        table_f = sb("table_f", [HALF, 4, P])
        table_hi = sb("table_hi", [HALF, 2, P], I32)
        table_row = sb("table_row", [HALF, 4, P], F16)
        src_f = sb("src_f", [P, TILES])
        src_i = sb("src_i", [P, TILES], I32)
        dst_i = sb("dst_i", [P, TILES], I32)
        part_i = sb("part_i", [P, 3, TILES], I32)
        lo_f = sb("lo_f", [P, TILES])
        dst_lo_f = sb("dst_lo_f", [P, TILES])
        hi_f = sb("hi_f", [P, TILES])
        src_less_spare = sb("src_less_spare", [P, TILES])
        iota_i = sb("iota_i", [P, HI], I32)
        iota_h = sb("iota_h", [P, HI], F16)
        ident = sb("ident", [P, P])
        later = sb("later", [P, GROUP * P])
        eps = sb("eps", [P, 1])
        chunk_id_i = sb("chunk_id_i", [P, CHUNKS], I32)
        chunk_id = sb("chunk_id", [P, CHUNKS])
        spare_i = sb("spare_i", [P, GROUP], I32)
        spare = sb("spare", [P, GROUP])
        comps_sb = sb("comps_sb", [R, B])
        alpha_sb = sb("alpha_sb", [R, 1])
        scaled_comps = sb("scaled_comps", [R, B])
        comps_rest = sb("comps_rest", [R, B])
        comps_split = sb("comps_split", [R, SPLITS, B], BF16)
        coef = sb("coef", [P, TILES, B])
        work = sb("work", [P, 7168])

        def part(start, size, dt=F32):
            return work[:, start:start + size].bitcast(dt) if dt != F32 else work[:, start:start + size]

        hot_size = GROUP * P
        lo_hot = part(0, hot_size, F16).rearrange("p (b j n) -> p b j n", b=2, j=GROUP)
        hi_hot = part(hot_size, GROUP * HI, F16).rearrange("p (b j n) -> p b j n", b=2, j=GROUP)
        degree = sb("degree", [P, HI])
        degree_turned = sb("degree_turned", [CH, CHUNKS, P])
        edge_row = sb("edge_row", [P, 2, 2, W], F16)
        node_hot = part(0, CHUNKS * W, F16).rearrange("p (b c e) -> p b c e", b=2, c=CHUNKS)
        type_hot = part(CHUNKS * W, W, BF16).rearrange("p (b e) -> p b e", b=2)
        degree_i = sb("degree_i", [CH, CHUNKS, P], I32)
        degree_parts = sb("degree_parts", [CH, PARTS, CHUNKS, P], F16)
        inverse_root = sb("inverse_root", [CH, CHUNKS, P])
        masked = sb("masked", [P, GROUP, P])
        picked = sb("picked", [P, 2, GROUP])
        gather_idx = sb("gather_idx", [P, 2, GROUP], I32)
        gathered = sb("gathered", [P, 2, GROUP, D])
        rows = sb("rows", [P, TILES, D])
        look_idx = sb("look_idx", [P, 2, GROUP], I32)
        looked = sb("looked", [P, 2, GROUP])
        dst_degree = sb("dst_degree", [P, TILES])
        dst_root = sb("dst_root", [P, TILES])
        src_norm = sb("src_norm", [P, TILES])
        stats = sb("stats", [P, TILES, 6])
        gap = sb("gap", [P, TILES])
        var = sb("var", [P, TILES])
        rstd = sb("rstd", [P, TILES])
        shift = sb("shift", [P, TILES])
        bases_sb = sb("bases_sb", [D, B, D])
        h = part(0, 2 * W).rearrange("p (b j d) -> p b j d", b=2, j=GROUP)
        h_turned = part(2 * W, 2 * W).rearrange("p (b j e) -> p b j e", b=2, j=GROUP)
        part_sum = part(4 * W, 2 * W).rearrange("p (b j d) -> p b j d", b=2, j=GROUP)
        src_row = sb("src_row", [P, 2, GROUP * P], I32)
        same = part(6 * W, 8 * W).rearrange("p (b j e) -> p b j e", b=2, j=GROUP)
        copies = sb("copies", [P, 2, GROUP])
        keep = sb("keep", [P, 2, GROUP])
        scatter_idx = sb("scatter_idx", [P, 2, GROUP], I32)
        sums = gathered

        pst = ctx.enter_context(nc.psum_tensor("pst", [P, 8, BANK], F32))

        copied = [sem(f"copied{b}") for b in range(2)]
        spare_filled = sem("spare_filled")
        tables_loaded = sem("tables_loaded")
        padded = sem("padded")
        weights_loaded = sem("weights_loaded")
        iota_ready = sem("iota_ready")
        ident_ready = sem("ident_ready")
        ident_cleared = sem("ident_cleared")
        dve_step = sem("dve_step")
        table_float = sem("table_float")
        table_turned = sem("table_turned")
        idx_ready = sem("idx_ready")
        hot_ready = sem("hot_ready")
        hot_used = sem("hot_used")
        degree_copied = sem("degree_copied")
        degree_turned_ps = sem("degree_turned_ps")
        degree_ready = sem("degree_ready")
        table_clamped = sem("table_clamped")
        table_root = sem("table_root")
        table_ready = sem("table_ready")
        inverse_ready = sem("inverse_ready")
        table_stored = sem("table_stored")
        row_table_ready = sem("row_table_ready")
        rows_stored = sem("rows_stored")
        edge_row_loaded = [sem(f"edge_row_loaded{b}") for b in range(2)]
        turned_hot_ready = sem("turned_hot_ready")
        look_ps = sem("look_ps")
        picked_ready = sem("picked_ready")
        degree_kept = sem("degree_kept")
        coef_kept = sem("coef_kept")
        idx_staged = sem("idx_staged")
        row_gathered = [sem(f"row_gathered{b}") for b in range(2)]
        rows_kept = sem("rows_kept")
        look_staged = sem("look_staged")
        look_done = [sem(f"look_done{b}") for b in range(2)]
        src_norm_ready = sem("src_norm_ready")
        stats_ready = sem("stats_ready")
        root_in = sem("root_in")
        root_done = sem("root_done")
        norm_ready = sem("norm_ready")
        h_ready = sem("h_ready")
        h_turned_ps = sem("h_turned_ps")
        h_turned_ready = sem("h_turned_ready")
        product_ready = sem("product_ready")
        first_part = sem("first_part")
        second_part = sem("second_part")
        third_part = sem("third_part")
        message_ready = sem("message_ready")
        src_row_loaded = [sem(f"src_row_loaded{b}") for b in range(2)]
        same_ready = sem("same_ready")
        keep_ready = sem("keep_ready")
        scatter_idx_ready = sem("scatter_idx_ready")
        sums_ps = sem("sums_ps")
        sums_ready = sem("sums_ready")
        scattered = sem("scattered")
        pool_turn = sem("pool_turn")

        def groups(body, eng, first=0, end=GROUPS):
            i = first
            while i < 2:
                body(i, i % 2)
                i += 1
            loop_end = min(end, GROUPS - 3)
            if loop_end > i:
                assert i % 2 == 0 and (loop_end - i) % 2 == 0
                with eng.Fori(i, loop_end - 1, 2) as k:
                    body(k, 0)
                    body(k + 1, 1)
                i = loop_end
            for j in range(i, end):
                body(j, j % 2)

        block = ctx.enter_context(nc.Block())

        @block.sync
        def _(sp):
            def load_table(slot, array):
                sp.dma_start(table_i[:, slot, :], array[0:HALF * P].rearrange("(t p) -> t p", p=P)) \
                    .then_inc(tables_loaded, 16)
                full = (HALF + LAST_ROWS) * P
                sp.dma_start(table_i[0:LAST_ROWS, slot + 1, :],
                             array[HALF * P:full].rearrange("(t p) -> t p", p=P)).then_inc(tables_loaded, 16)
                sp.dma_start(table_i[LAST_ROWS:LAST_ROWS + 1, slot + 1, 0:LAST_EDGES],
                             array[full:E].rearrange("(t p) -> t p", t=1)).then_inc(tables_loaded, 16)

            sp.wait_ge(padded, 4)
            load_table(0, dst)
            load_table(2, src)
            load_table(4, edge_type)
            sp.dma_start(comps_sb[:], comps).then_inc(weights_loaded, 16)
            sp.dma_start(alpha_sb[:], alpha).then_inc(weights_loaded, 16)
            sp.dma_start(bases_sb[:], bases.rearrange("b d f -> d b f")).then_inc(weights_loaded, 16)
            extra = out.shape[0] - N
            sp.dma_start(out[N:N + extra, :], x[0:extra, :]).then_inc(spare_filled, 16)
            sp.wait_ge(row_table_ready, 2)
            for k in range(2):
                sp.dma_start(edge_row_dram[k, :].rearrange("(h t p) -> t h p", h=2, p=P),
                             table_row[:, 2 * k:2 * k + 2, :]).then_inc(rows_stored, 16)

            def copy(i, b):
                if not (isinstance(i, int) and i < 2):
                    sp.wait_ge(copied[b], (i - b) * 8)
                a = i * COPY_ROWS
                flat_out, flat_x = (y[bass.ds(a, COPY_ROWS), :].rearrange("r d -> (r d)") for y in (out, x))
                sp.dma_start(flat_out.rearrange("(q e) -> q e", q=16), flat_x.rearrange("(q e) -> q e", q=16)) \
                    .then_inc(copied[b], 16)

            copy(0, 0)
            copy(1, 1)
            with sp.Fori(2, EARLY_COPIES - 1, 2) as k:
                copy(k, 0)
                copy(k + 1, 1)
            sp.wait_ge(rows_stored, 32)

            def load_edge_row(i, b):
                if not (isinstance(i, int) and i < 2):
                    sp.wait_ge(turned_hot_ready, i - 1)
                sp.dma_start(edge_row[:, b, :, :],
                             edge_row_dram[:, bass.ds(i * W, W)].rearrange("(o k) e -> o k e", o=1)
                             .to_broadcast([P, 2, W])).then_inc(edge_row_loaded[b], 16)

            load_edge_row(0, 0)
            load_edge_row(1, 1)
            with sp.Fori(1, (GROUPS - 1) // 2) as k:
                load_edge_row(2 * k, 0)
                load_edge_row(2 * k + 1, 1)
                copy(EARLY_COPIES - 2 + 2 * k, 0)
                copy(EARLY_COPIES - 1 + 2 * k, 1)
            load_edge_row(GROUPS - 1, 0)

            def load_src_row(i, b):
                last = isinstance(i, int) and i == GROUPS - 1
                if not (isinstance(i, int) and i < 2):
                    sp.wait_ge(same_ready, GROUP * (i - 1))
                n = LAST_GROUP if last else GROUP * P
                sp.dma_start(src_row[:, b, 0:n],
                             src[bass.ds(i * (GROUP * P), n)].rearrange("(o e) -> o e", o=1).to_broadcast([P, n])) \
                    .then_inc(src_row_loaded[b], 16)

            groups(load_src_row, sp)
            sp.wait_ge(spare_filled, 16)
            for b in range(2):
                sp.wait_ge(copied[b], 8 * COPIES)
            sp.wait_ge(rows_stored, 32)
            sp.wait_ge(table_stored, 16)
            sp.wait_ge(scattered, 16 * TILES)

        @block.gpsimd
        def _(pool):
            pool.iota(iota_i[:], [[1, HI]], base=0, channel_multiplier=0).then_inc(iota_ready, 1)
            pool.iota(chunk_id_i[:], [[CH, CHUNKS]], base=0, channel_multiplier=1).then_inc(iota_ready, 1)
            pool.iota(spare_i[:], [[P, GROUP]], base=SPARE, channel_multiplier=1).then_inc(iota_ready, 1)
            pool.memset(ident[:], 0.0).then_inc(ident_cleared, 1)
            pool.memset(later[:], 1.0).then_inc(ident_cleared, 1)
            pool.wait_ge(ident_cleared, 2)
            pool.affine_select(out=ident[:], in_=ident[:], compare_op=ALU.not_equal, fill=1.0, base=0,
                               pattern=[[-1, P]], channel_multiplier=1).then_inc(ident_ready, 1)
            pool.affine_select(out=later[:, 0:P], in_=later[:, 0:P], compare_op=ALU.is_ge, fill=0.0, base=0,
                               pattern=[[1, P]], channel_multiplier=-1).then_inc(ident_ready, 1)

            pool.wait_ge(idx_ready, 1)

            def gather_rows(i, b):
                if not (isinstance(i, int) and i < 2):
                    pool.wait_ge(rows_kept, i - 1)
                pool.tensor_copy(gather_idx[:, b, :], dst_i[:, bass.ds(i * GROUP, GROUP)]).then_inc(idx_staged, 1)
                pool.wait_ge(idx_staged, i + 1)
                pool.sem_inc(pool_turn)
                for j in range(GROUP):
                    pool.indirect_dma_start(gathered[:, b, j, :], None, x,
                                            bass.IndirectOffsetOnAxis(ap=gather_idx[:, b, j:j + 1], axis=0)) \
                        .then_inc(row_gathered[b], 16)

            groups(gather_rows, pool)

            pool.wait_ge(table_stored, 16)
            pool.wait_ge(idx_ready, 2)

            def keep_looked(i, b):
                pool.wait_ge(look_done[b], (i - b) * (8 * GROUP) + 16 * GROUP)
                pool.tensor_copy(src_norm[:, bass.ds(i * GROUP, GROUP)], looked[:, b, :]).then_inc(src_norm_ready, 1)

            def look_up(i, b):
                if not (isinstance(i, int) and i < 2):
                    keep_looked(i - 2, b)
                pool.tensor_copy(look_idx[:, b, :], src_i[:, bass.ds(i * GROUP, GROUP)]).then_inc(look_staged, 1)
                if not (isinstance(i, int) and i < 2):
                    pool.wait_ge(src_norm_ready, i - 1)
                pool.wait_ge(look_staged, i + 1)
                pool.sem_inc(pool_turn)
                for j in range(GROUP):
                    pool.indirect_dma_start(looked[:, b, j:j + 1], None, inverse_root_dram,
                                            bass.IndirectOffsetOnAxis(ap=look_idx[:, b, j:j + 1], axis=0)) \
                        .then_inc(look_done[b], 16)

            def scatter(i, b):
                pool.wait_ge(scatter_idx_ready, i + 1)
                pool.wait_ge(sums_ready, GROUP * (i + 1))
                if not (isinstance(i, int) and i == 0):
                    pool.wait_ge(scattered, 16 * GROUP * i)
                pool.sem_inc(pool_turn)
                for j in range(GROUP):
                    pool.indirect_dma_start(out, bass.IndirectOffsetOnAxis(ap=scatter_idx[:, b, j:j + 1], axis=0),
                                            sums[:, b, j, :], None, bounds_check=out.shape[0] - 1,
                                            oob_is_err=True, compute_op=ALU.add).then_inc(scattered, 16)

            groups(look_up, pool, 0, LEAD)
            pool.wait_ge(spare_filled, 16)
            for b in range(2):
                pool.wait_ge(copied[b], 8 * COPIES)

            def scatter_and_look_up(i, b):
                scatter(i, b)
                look_up(i + LEAD, b)

            groups(scatter_and_look_up, pool, 0, GROUPS - 1 - LEAD)
            scatter(GROUPS - 1 - LEAD, (GROUPS - 1 - LEAD) % 2)
            look_up(GROUPS - 1, 0)
            keep_looked(GROUPS - 2, 1)
            keep_looked(GROUPS - 1, 0)
            scatter(GROUPS - LEAD, (GROUPS - LEAD) % 2)
            groups(scatter, pool, GROUPS - LEAD + 1, GROUPS)

        @block.vector
        def _(dve):
            steps = [0]

            def step(ins):
                steps[0] += 1
                ins.then_inc(dve_step, 1)
                dve.wait_ge(dve_step, steps[0])

            dve.memset(table_i[:, 1, :], 0).then_inc(padded, 1)
            dve.memset(table_i[:, 3, :], PAD_NODE).then_inc(padded, 1)
            dve.memset(table_i[:, 5, :], 0).then_inc(padded, 1)
            dve.memset(eps[:], EPS).then_inc(padded, 1)
            dve.wait_ge(iota_ready, 3)
            dve.tensor_copy(iota_h[:], iota_i[:])
            dve.tensor_copy(chunk_id[:], chunk_id_i[:])
            step(dve.tensor_copy(spare[:], spare_i[:]))
            dve.wait_ge(tables_loaded, 16 * 9)
            dve.tensor_copy(table_f[:], table_i[:, 0:4, :]).then_inc(table_float, 1)
            step(dve.tensor_scalar(table_hi[:], table_i[:, 0:2, :], P.bit_length() - 1, None,
                                   ALU.logical_shift_right))
            dve.tensor_copy(table_row[:, 0:2, :], table_hi[:]).then_inc(row_table_ready, 1)
            dve.tensor_copy(table_row[:, 2:4, :], table_i[:, 4:6, :]).then_inc(row_table_ready, 1)
            dve.wait_ge(table_turned, 1)
            turned = pst[:, 2, 0:4 * HALF].rearrange("p (k t) -> p k t", k=4)
            dve.tensor_copy(dst_i[:].rearrange("p (k t) -> p k t", k=2), turned[:, 0:2, :]).then_inc(idx_ready, 1)
            dve.wait_ge(idx_ready, 1)
            step(dve.tensor_copy(src_i[:].rearrange("p (k t) -> p k t", k=2), turned[:, 2:4, :]))
            step(dve.tensor_copy(src_f[:].rearrange("p (k t) -> p k t", k=2), turned[:, 2:4, :]))
            step(dve.tensor_scalar(part_i[:, 0, :], src_i[:], P.bit_length() - 1, None, ALU.logical_shift_right))
            step(dve.tensor_scalar(part_i[:, 1, :], src_i[:], P - 1, None, ALU.bitwise_and))
            step(dve.tensor_scalar(part_i[:, 2, :], dst_i[:], P - 1, None, ALU.bitwise_and))
            dve.tensor_copy(hi_f[:], part_i[:, 0, :])
            dve.tensor_copy(dst_lo_f[:], part_i[:, 2, :])
            step(dve.tensor_copy(lo_f[:], part_i[:, 1, :]))
            step(dve.tensor_tensor(src_less_spare[:].rearrange("p (g j) -> p g j", j=GROUP),
                                   src_f[:].rearrange("p (g j) -> p g j", j=GROUP),
                                   spare[:].rearrange("p (g j) -> p g j", g=1).to_broadcast([P, GROUPS, GROUP]),
                                   ALU.subtract))
            dve.nop().then_inc(idx_ready, 1)

            def hots(i, b):
                if not (isinstance(i, int) and i < 2):
                    dve.wait_ge(hot_used, GROUP * (i - 1))
                for j in range(GROUP):
                    t = i * GROUP + j
                    dve.tensor_scalar(lo_hot[:, b, j, :], iota_h[:, 0:P], lo_f[:, bass.ds(t, 1)], None,
                                      ALU.is_equal)
                    dve.tensor_scalar(hi_hot[:, b, j, :], iota_h[:], hi_f[:, bass.ds(t, 1)], None,
                                      ALU.is_equal).then_inc(hot_ready, 1)

            groups(hots, dve)
            dve.wait_ge(hot_used, TILES)
            dve.tensor_copy(degree[:, 0:BANK], pst[:, 0, :]).then_inc(degree_copied, 1)
            dve.tensor_copy(degree[:, BANK:HI], pst[:, 1, 0:HI - BANK]).then_inc(degree_copied, 1)
            for c in range(CHUNKS):
                dve.wait_ge(degree_turned_ps, min(c - c % 4 + 4, CHUNKS))
                dve.tensor_copy(degree_turned[:, c, :], pst[0:CH, 3 + c // 4, (c % 4) * P:(c % 4 + 1) * P]) \
                    .then_inc(degree_ready, 1)

            dve.wait_ge(degree_ready, CHUNKS)
            dve.tensor_scalar(inverse_root[:], degree_turned[:], 1.0, None, ALU.max).then_inc(table_clamped, 1)
            step(dve.tensor_copy(degree_i[:], degree_turned[:]))
            step(dve.tensor_scalar(degree_i[:], degree_i[:], LOW - 1, None, ALU.bitwise_and))
            step(dve.tensor_copy(degree_parts[:, 0, :, :], degree_i[:]))
            step(dve.tensor_tensor(degree_parts[:, 1, :, :], degree_turned[:], degree_parts[:, 0, :, :],
                                   ALU.subtract))
            dve.wait_ge(weights_loaded, 16 * 3)
            step(dve.tensor_scalar(comps_rest[:], comps_sb[:], alpha_sb[:, 0:1], None, ALU.mult))
            for k in range(SPLITS):
                step(dve.tensor_copy(comps_split[:, k, :], comps_rest[:]))
                if k < SPLITS - 1:
                    step(dve.tensor_tensor(comps_rest[:], comps_rest[:], comps_split[:, k, :], ALU.subtract))
            dve.nop().then_inc(table_ready, 1)

            def turned_hots(i, b):
                dve.wait_ge(edge_row_loaded[b], (i - b) * 8 + 16)
                if not (isinstance(i, int) and i < 2):
                    dve.wait_ge(look_ps, i - 1)
                for c in range(CHUNKS):
                    dve.tensor_scalar(node_hot[0:CH, b, c, :], edge_row[0:CH, b, 0, :], chunk_id[0:CH, c:c + 1], None,
                                      ALU.is_equal)
                dve.tensor_scalar(type_hot[0:R, b, :], edge_row[0:R, b, 1, :], chunk_id[0:R, 0:1], None,
                                  ALU.is_equal).then_inc(turned_hot_ready, 1)

            def pick(i, b):
                dve.wait_ge(look_ps, i + 1)
                for j in range(GROUP):
                    dve.scalar_tensor_tensor(out=masked[:, j, :], in0=iota_h[:, 0:P],
                                             scalar=dst_lo_f[:, bass.ds(i * GROUP + j, 1)],
                                             in1=pst[:, 2 + b, j * P:(j + 1) * P], op0=ALU.is_equal, op1=ALU.mult,
                                             accum_out=picked[:, b, j:j + 1]).then_inc(picked_ready, 1)
                dve.tensor_copy(coef[:, bass.ds(i * GROUP, GROUP), :].rearrange("p t b -> p (t b)"),
                                pst[:, 4 + b, 0:GROUP * B]).then_inc(coef_kept, 1)
                dve.wait_ge(picked_ready, GROUP * (i + 1))
                dve.tensor_copy(dst_degree[:, bass.ds(i * GROUP, GROUP)], picked[:, b, :]).then_inc(degree_kept, 1)

            def look(i, b):
                turned_hots(i, b)
                if not (isinstance(i, int) and i < 1):
                    pick(i - 1, 1 - b)

            groups(look, dve, 0, INVERT_AT)
            dve.wait_ge(table_root, 1)
            step(dve.reciprocal(inverse_root[:], inverse_root[:]))
            dve.scalar_tensor_tensor(out=inverse_root[:], in0=degree_turned[:], scalar=1.0, in1=inverse_root[:],
                                     op0=ALU.min, op1=ALU.mult).then_inc(inverse_ready, 1)
            groups(look, dve, INVERT_AT, GROUPS)
            pick(GROUPS - 1, 0)

            def row_stats(i, b):
                dve.wait_ge(rows_kept, i + 1)
                for j in range(GROUP):
                    t = i * GROUP + j
                    last = dve.bn_stats(stats[:, bass.ds(t, 1), :].rearrange("p a s -> p (a s)"),
                                        rows[:, bass.ds(t, 1), :].rearrange("p a d -> p (a d)"))
                last.then_inc(stats_ready, 1)

            groups(row_stats, dve)
            dve.wait_ge(stats_ready, GROUPS)
            mean0, spread0, mean1, spread1 = (stats[:, :, k] for k in (1, 2, 4, 5))
            step(dve.tensor_tensor(gap[:], mean0, mean1, ALU.subtract))
            step(dve.tensor_tensor(gap[:], gap[:], gap[:], ALU.mult))
            step(dve.tensor_tensor(var[:], spread0, spread1, ALU.add))
            step(dve.scalar_tensor_tensor(out=var[:], in0=gap[:], scalar=D / 4, in1=var[:], op0=ALU.mult,
                                          op1=ALU.add))
            step(dve.tensor_tensor(shift[:], mean0, mean1, ALU.add))
            dve.nop().then_inc(root_in, 1)
            dve.wait_ge(root_done, 1)
            step(dve.reciprocal(rstd[:], rstd[:]))
            step(dve.scalar_tensor_tensor(out=shift[:], in0=shift[:], scalar=-0.5, in1=rstd[:], op0=ALU.mult,
                                          op1=ALU.mult))
            dve.nop().then_inc(norm_ready, 1)

            dve.wait_ge(degree_kept, GROUPS)
            step(dve.tensor_scalar(dst_root[:], dst_degree[:], 1.0, None, ALU.max))
            dve.nop().then_inc(root_in, 1)
            dve.wait_ge(root_done, 2)
            step(dve.reciprocal(dst_root[:], dst_root[:]))
            step(dve.scalar_tensor_tensor(out=dst_root[:], in0=dst_degree[:], scalar=1.0, in1=dst_root[:],
                                          op0=ALU.min, op1=ALU.mult))
            dve.wait_ge(coef_kept, GROUPS)
            step(dve.tensor_tensor(coef[:], coef[:], dst_root[:].rearrange("p (t o) -> p t o", o=1)
                                   .to_broadcast([P, TILES, B]), ALU.mult))
            dve.nop().then_inc(norm_ready, 1)

            def messages(i, b):
                for j in range(GROUP):
                    t = i * GROUP + j
                    u = pst[:, 4 + j, :].rearrange("p (b f) -> p b f", b=B)
                    c = coef[:, bass.ds(t, 1), :].rearrange("p a b -> p (a b)")
                    dve.wait_ge(first_part, t + 1)
                    dve.scalar_tensor_tensor(out=part_sum[:, b, j, :], in0=u[:, 1, :], scalar=c[:, 1:2],
                                             in1=part_sum[:, b, j, :], op0=ALU.mult, op1=ALU.add) \
                        .then_inc(second_part, 1)
                for j in range(GROUP):
                    t = i * GROUP + j
                    u = pst[:, 4 + j, :].rearrange("p (b f) -> p b f", b=B)
                    c = coef[:, bass.ds(t, 1), :].rearrange("p a b -> p (a b)")
                    dve.wait_ge(second_part, t + 1)
                    dve.scalar_tensor_tensor(out=part_sum[:, b, j, :], in0=u[:, 2, :], scalar=c[:, 2:3],
                                             in1=part_sum[:, b, j, :], op0=ALU.mult, op1=ALU.add) \
                        .then_inc(third_part, 1)
                for j in range(GROUP):
                    t = i * GROUP + j
                    u = pst[:, 4 + j, :].rearrange("p (b f) -> p b f", b=B)
                    c = coef[:, bass.ds(t, 1), :].rearrange("p a b -> p (a b)")
                    dve.wait_ge(third_part, t + 1)
                    dve.scalar_tensor_tensor(out=rows[:, bass.ds(t, 1), :].rearrange("p a d -> p (a d)"),
                                             in0=u[:, 3, :], scalar=c[:, 3:4],
                                             in1=part_sum[:, b, j, :], op0=ALU.mult, op1=ALU.add) \
                        .then_inc(message_ready, 1)

            def same_src(i, b):
                if isinstance(i, int) and i == GROUPS - 1:
                    dve.wait_ge(same_ready, GROUP * (GROUPS - 2))
                    dve.memset(src_row[:, b, LAST_GROUP:], PAD_NODE).then_inc(padded, 1)
                    dve.wait_ge(padded, 5)
                dve.wait_ge(src_row_loaded[b], 16 * ((i - b) // 2 + 1) if isinstance(i, int) else
                            (i - b) * 8 + 16)
                if not (isinstance(i, int) and i < 2):
                    dve.wait_ge(sums_ps, i - 1)
                    dve.wait_ge(scattered, 16 * GROUP * (i - 1))
                for j in range(GROUP):
                    t = i * GROUP + j
                    w = (GROUP - j) * P
                    dve.scalar_tensor_tensor(out=same[:, b, j, 0:w], in0=src_row[:, b, j * P:],
                                             scalar=src_f[:, bass.ds(t, 1)], in1=later[:, 0:w],
                                             op0=ALU.is_equal, op1=ALU.mult,
                                             accum_out=copies[:, b, j:j + 1]).then_inc(same_ready, 1)
                dve.wait_ge(same_ready, GROUP * (i + 1))
                dve.scalar_tensor_tensor(out=keep[:, b, :], in0=copies[:, b, :], scalar=1.0,
                                         in1=src_less_spare[:, bass.ds(i * GROUP, GROUP)], op0=ALU.is_equal,
                                         op1=ALU.mult).then_inc(keep_ready, 1)
                dve.wait_ge(keep_ready, i + 1)
                dve.tensor_tensor(scatter_idx[:, b, :], keep[:, b, :], spare[:], ALU.add) \
                    .then_inc(scatter_idx_ready, 1)

            def messages_and_same(i, b):
                messages(i, b)
                same_src(i, b)

            groups(messages_and_same, dve)

        @block.scalar
        def _(act):
            def keep_rows(i, b):
                act.wait_ge(row_gathered[b], (i - b) * (8 * GROUP) + 16 * GROUP)
                act.activation(rows[:, bass.ds(i * GROUP, GROUP), :].rearrange("p t d -> p (t d)"),
                               gathered[:, b, :, :].rearrange("p t d -> p (t d)"), ACT.Copy) \
                    .then_inc(rows_kept, 1)

            groups(keep_rows, act, 0, ROOT_AT)
            act.wait_ge(table_clamped, 1)
            act.activation(inverse_root[:], inverse_root[:], ACT.Sqrt).then_inc(table_root, 1)
            groups(keep_rows, act, ROOT_AT, STORE_AT)
            act.wait_ge(inverse_ready, 1)
            act.dma_start(inverse_root_dram.rearrange("(c r l) o -> r c (l o)", c=CHUNKS, l=P), inverse_root[:]) \
                .then_inc(table_stored, 16)
            groups(keep_rows, act, STORE_AT, GROUPS)

            act.wait_ge(root_in, 1)
            act.activation(rstd[:], var[:], ACT.Sqrt, bias=eps[:, 0:1], scale=1.0 / D).then_inc(root_done, 1)
            act.wait_ge(root_in, 2)
            act.activation(dst_root[:], dst_root[:], ACT.Sqrt).then_inc(root_done, 1)

            def relu(i, b):
                if not (isinstance(i, int) and i < 2):
                    act.wait_ge(h_turned_ps, i - 1)
                for j in range(GROUP):
                    t = i * GROUP + j
                    last = act.activation(h[:, b, j, :], rows[:, bass.ds(t, 1), :].rearrange("p a d -> p (a d)"),
                                          ACT.Relu, bias=shift[:, bass.ds(t, 1)], scale=rstd[:, bass.ds(t, 1)])
                last.then_inc(h_ready, 1)

            def keep_turned(i, b):
                act.wait_ge(h_turned_ps, i + 1)
                if not (isinstance(i, int) and i < 2):
                    act.wait_ge(product_ready, GROUP * (i - 1))
                act.activation(h_turned[:, b, :, :].rearrange("p t e -> p (t e)"), pst[:, 2 + b, :], ACT.Copy) \
                    .then_inc(h_turned_ready, 1)

            def first(i, b, j):
                t = i * GROUP + j
                act.wait_ge(product_ready, t + 1)
                if not (isinstance(i, int) and i < 2):
                    act.wait_ge(message_ready, GROUP * (i - 1))
                act.activation(part_sum[:, b, j, :], pst[:, 4 + j, 0:D], ACT.Copy,
                               scale=coef[:, bass.ds(t, 1), :].rearrange("p a b -> p (a b)")[:, 0:1]) \
                    .then_inc(first_part, 1)

            act.wait_ge(norm_ready, 2)
            relu(0, 0)
            relu(1, 1)
            keep_turned(0, 0)

            def transform(i, b):
                first(i, b, 0)
                first(i, b, 1)
                if not (isinstance(i, int) and i + 1 >= GROUPS):
                    keep_turned(i + 1, 1 - b)
                if not (isinstance(i, int) and i + 2 >= GROUPS):
                    relu(i + 2, b)
                first(i, b, 2)
                first(i, b, 3)

            def scale_sums(i, b):
                act.wait_ge(sums_ps, i + 1)
                act.wait_ge(src_norm_ready, i + 1)
                if not (isinstance(i, int) and i < 2):
                    act.wait_ge(scattered, 16 * GROUP * (i - 1))
                for j in range(GROUP):
                    act.activation(sums[:, b, j, :], pst[:, b, j * P:(j + 1) * P], ACT.Copy,
                                   scale=src_norm[:, bass.ds(i * GROUP + j, 1)]).then_inc(sums_ready, 1)

            def transform_and_scale(i, b):
                transform(i, b)
                if not (isinstance(i, int) and i < 1):
                    scale_sums(i - 1, 1 - b)

            groups(transform_and_scale, act)
            scale_sums(GROUPS - 1, 0)

        @block.tensor
        def _(pe):
            pe.wait_ge(ident_ready, 2)
            pe.wait_ge(table_float, 1)
            for k in range(4):
                last = pe.transpose(pst[:, 2, k * HALF:(k + 1) * HALF], table_f[:, k, :], ident[0:HALF, 0:HALF])
            last.then_inc(table_turned, 1)

            def histogram(i, b):
                for j in range(GROUP):
                    t = i * GROUP + j
                    start = isinstance(i, int) and i == 0 and j == 0
                    stop = isinstance(i, int) and i == GROUPS - 1 and j == GROUP - 1
                    pe.wait_ge(hot_ready, t + 1)
                    pe.matmul(pst[:, 0, :], lo_hot[:, b, j, :], hi_hot[:, b, j, 0:BANK], start=start, stop=stop)
                    pe.matmul(pst[:, 1, 0:HI - BANK], lo_hot[:, b, j, :], hi_hot[:, b, j, BANK:HI],
                              start=start, stop=stop).then_inc(hot_used, 1)

            groups(histogram, pe)
            pe.wait_ge(degree_copied, 2)
            for c in range(CHUNKS):
                pe.transpose(pst[0:CH, 3 + c // 4, (c % 4) * P:(c % 4 + 1) * P], degree[:, c * CH:(c + 1) * CH],
                             ident[:]).then_inc(degree_turned_ps, 1)

            pe.wait_ge(table_ready, 1)

            def look(i, b):
                pe.wait_ge(turned_hot_ready, i + 1)
                if not (isinstance(i, int) and i < 2):
                    pe.wait_ge(picked_ready, GROUP * (i - 1))
                    pe.wait_ge(coef_kept, i - 1)
                for j in range(GROUP):
                    for c in range(CHUNKS):
                        for k in range(PARTS):
                            pe.matmul(pst[:, 2 + b, j * P:(j + 1) * P], node_hot[0:CH, b, c, j * P:(j + 1) * P],
                                      degree_parts[:, k, c, :], start=(c == 0 and k == 0),
                                      stop=(c == CHUNKS - 1 and k == PARTS - 1))
                    for k in range(SPLITS):
                        last = pe.matmul(pst[:, 4 + b, j * B:(j + 1) * B], type_hot[0:R, b, j * P:(j + 1) * P],
                                         comps_split[:, k, :], start=(k == 0), stop=(k == SPLITS - 1))
                last.then_inc(look_ps, 1)

            groups(look, pe)

            def turn(i, b):
                pe.wait_ge(h_ready, i + 1)
                if not (isinstance(i, int) and i < 2):
                    pe.wait_ge(h_turned_ready, i - 1)
                for j in range(GROUP):
                    last = pe.transpose(pst[:, 2 + b, j * P:(j + 1) * P], h[:, b, j, :], ident[:])
                last.then_inc(h_turned_ps, 1)

            def multiply(i, b):
                if not (isinstance(i, int) and i + 1 >= GROUPS):
                    turn(i + 1, 1 - b)
                pe.wait_ge(h_turned_ready, i + 1)
                for j in range(GROUP):
                    if not (isinstance(i, int) and i < 1):
                        pe.wait_ge(message_ready, (i - 1) * GROUP + j + 1)
                    pe.matmul(pst[:, 4 + j, :], h_turned[:, b, j, :], bases_sb[:].rearrange("d b f -> d (b f)"),
                              start=True, stop=True).then_inc(product_ready, 1)

            def add_same(i, b):
                pe.wait_ge(same_ready, GROUP * (i + 1))
                pe.wait_ge(message_ready, GROUP * (i + 1))
                if not (isinstance(i, int) and i < 2):
                    pe.wait_ge(sums_ready, GROUP * (i - 1))
                for t in range(GROUP):
                    for s in range(t + 1):
                        last = pe.matmul(pst[:, b, t * P:(t + 1) * P], same[:, b, s, (t - s) * P:(t - s + 1) * P],
                                         rows[:, bass.ds(i * GROUP + s, 1), :].rearrange("p a d -> p (a d)"),
                                         start=(s == 0), stop=(s == t))
                last.then_inc(sums_ps, 1)

            def multiply_and_add(i, b):
                multiply(i, b)
                if not (isinstance(i, int) and i < 1):
                    add_same(i - 1, 1 - b)

            turn(0, 0)
            groups(multiply_and_add, pe)
            add_same(GROUPS - 1, 0)


_INS = ['x', 'src', 'dst', 'edge_type_50', 'L0_gnn_bases', 'L0_gnn_comps', 'L0_gnn_alpha']


def kernel(**inputs):
    import numpy as _np
    import concourse.bacc as _bacc
    from concourse import mybir as _mybir
    from concourse.bass_utils import run_bass_kernel_spmd as _run

    nc = _bacc.Bacc("TRN2", target_bir_lowering=False, num_devices=1)
    arrays, args = {}, []
    for name in _INS:
        a = _np.ascontiguousarray(inputs[name])
        arrays[f"in_{name}_dram"] = a
        args.append(nc.dram_tensor(f"in_{name}_dram", a.shape, _mybir.dt.from_np(a.dtype), kind="ExternalInput").ap())
    nodes, width = inputs["x"].shape
    args.append(nc.dram_tensor("out_dram", (padded_rows(nodes), width), _mybir.dt.float32,
                               kind="ExternalOutput").ap())
    build(nc, *args)
    r = _run(nc, [arrays], core_ids=[0])
    return r.results[0]["out_dram"][:nodes]
```

```python
from contextlib import ExitStack

import concourse.bass as bass
from concourse import mybir

ALU = mybir.AluOpType
ACT = mybir.ActivationFunctionType
F32 = mybir.dt.float32
F16 = mybir.dt.float16
BF16 = mybir.dt.bfloat16
I32 = mybir.dt.int32

P = 128
GROUP = 4
EPS = 1e-5


def padded_rows(nodes):
    return -(-(nodes + GROUP * P + 1) // P) * P


def build(nc, x, src, dst, edge_type, bases, comps, alpha, out):
    N, D = x.shape
    E = src.shape[0]
    R, B = comps.shape
    TILES = -(-E // P)
    GROUPS = TILES // GROUP
    HALF = TILES // 2
    assert D == P and TILES == GROUPS * GROUP and TILES == 2 * HALF and HALF <= P and GROUPS % 2 == 1
    LAST_ROWS = E // P - HALF
    LAST_EDGES = E % P
    LAST_GROUP = E - (GROUPS - 1) * GROUP * P
    SPARE = N
    PAD_NODE = N + GROUP * P
    CHUNKS = 7
    CH = -(-(PAD_NODE // P + 1) // CHUNKS)
    CH += CH % 2
    HI = CHUNKS * CH
    BANK = 512
    PARTS = 2
    LOW = 2048
    SPLITS = 3
    COPIES = 2 * (GROUPS + 1)
    COPY_ROWS = N // COPIES
    AHEAD = 28
    EARLY_COPIES = COPIES - 4 * (AHEAD // 2 - 1)
    ROOT_AT, STORE_AT = 24, 34
    INVERT_AT = 8
    LEAD, QUICK, EVEN = 12, 2, 12
    SPARSE = (GROUPS - 1 - LEAD - 6 * QUICK - EVEN) // 2
    SPARSE_AT = 4 * QUICK + EVEN
    ALONE_AT = SPARSE_AT + 4 * SPARSE
    assert LEAD % 2 == EVEN % 2 == 0 and ALONE_AT <= GROUPS - 5
    W = GROUP * P
    LO_TILES = 2
    HIST_LO, HIST_HI = LO_TILES * P, HI // LO_TILES
    assert HI % LO_TILES == 0 and HIST_HI <= BANK
    assert COPY_ROWS * COPIES == N and E < PARTS * LOW * LOW

    inverse_root_dram = nc.dram_tensor("inverse_root_table", (HI * P, 1), F32, kind="Internal").ap()
    edge_row_dram = nc.dram_tensor("edge_rows", (2, TILES * P), F16, kind="Internal").ap()

    with ExitStack() as ctx:
        def sb(name, shape, dt=F32):
            return ctx.enter_context(nc.sbuf_tensor(name, shape, dt))

        def sem(name):
            return ctx.enter_context(nc.semaphore(name))

        table_i = sb("table_i", [HALF, 6, P], I32)
        table_f = sb("table_f", [HALF, 4, P])
        table_hi = sb("table_hi", [HALF, 2, P], I32)
        table_row = sb("table_row", [HALF, 4, P], F16)
        src_f = sb("src_f", [P, TILES])
        src_i = sb("src_i", [P, TILES], I32)
        dst_i = sb("dst_i", [P, TILES], I32)
        part_i = sb("part_i", [P, 3, TILES], I32)
        lo_f = sb("lo_f", [P, TILES])
        dst_lo_f = sb("dst_lo_f", [P, TILES])
        hi_f = sb("hi_f", [P, TILES])
        src_less_spare = sb("src_less_spare", [P, TILES])
        iota_i = sb("iota_i", [P, HI], I32)
        iota_h = sb("iota_h", [P, HI], F16)
        ident = sb("ident", [P, P])
        later = sb("later", [P, GROUP * P])
        eps = sb("eps", [P, 1])
        chunk_id_i = sb("chunk_id_i", [P, CHUNKS], I32)
        chunk_id = sb("chunk_id", [P, CHUNKS])
        spare_i = sb("spare_i", [P, GROUP], I32)
        spare = sb("spare", [P, GROUP])
        comps_sb = sb("comps_sb", [R, B])
        alpha_sb = sb("alpha_sb", [R, 1])
        scaled_comps = sb("scaled_comps", [R, B])
        comps_rest = sb("comps_rest", [R, B])
        comps_split = sb("comps_split", [R, SPLITS, B], BF16)
        coef = sb("coef", [P, TILES, B])
        work = sb("work", [P, 14 * W + CHUNKS * W + W])

        def part(start, size, dt=F32):
            return work[:, start:start + size].bitcast(dt) if dt != F32 else work[:, start:start + size]

        hot_size = GROUP * HIST_LO
        lo_hot = part(0, hot_size, F16).rearrange("p (b j n) -> p b j n", b=2, j=GROUP)
        hi_hot = part(hot_size, GROUP * HIST_HI, F16).rearrange("p (b j n) -> p b j n", b=2, j=GROUP)
        degree = part(hot_size + GROUP * HIST_HI, HI)
        degree_turned = sb("degree_turned", [CH, CHUNKS, P])
        edge_row = sb("edge_row", [P, 2, 2, W], F16)
        node_hot = part(14 * W, CHUNKS * W, F16).rearrange("p (b c e) -> p b c e", b=2, c=CHUNKS)
        type_hot = part((14 + CHUNKS) * W, W, BF16).rearrange("p (b e) -> p b e", b=2)
        degree_i = part(hot_size + GROUP * HIST_HI + HI, CHUNKS * P)[0:CH, :].bitcast(I32).rearrange(
            "p (c l) -> p c l", c=CHUNKS)
        degree_parts = sb("degree_parts", [CH, PARTS, CHUNKS, P], F16)
        inverse_root = sb("inverse_root", [CH, CHUNKS, P])
        masked = sb("masked", [P, GROUP, P])
        picked = sb("picked", [P, 2, GROUP])
        gather_idx = sb("gather_idx", [P, 2, GROUP], I32)
        gathered = sb("gathered", [P, 2, GROUP, D])
        rows = sb("rows", [P, TILES, D])
        look_idx = sb("look_idx", [P, 2, GROUP], I32)
        looked = sb("looked", [P, 2, GROUP])
        dst_degree = sb("dst_degree", [P, TILES])
        dst_root = sb("dst_root", [P, TILES])
        src_norm = sb("src_norm", [P, TILES])
        row_sum = sb("row_sum", [P, 2, GROUP])
        row_squares = sb("row_squares", [P, 2, GROUP])
        mean = sb("mean", [P, 2, GROUP])
        squared = sb("squared", [P, GROUP, D])
        squares = sb("squares", [P, TILES])
        rstd = sb("rstd", [P, TILES])
        shift = sb("shift", [P, TILES])
        bases_sb = sb("bases_sb", [D, B, D])
        h = part(0, 2 * W).rearrange("p (b j d) -> p b j d", b=2, j=GROUP)
        h_turned = part(2 * W, 2 * W).rearrange("p (b j e) -> p b j e", b=2, j=GROUP)
        part_sum = part(4 * W, 2 * W).rearrange("p (b j d) -> p b j d", b=2, j=GROUP)
        src_row = sb("src_row", [P, 2, GROUP * P], I32)
        same = part(6 * W, 8 * W).rearrange("p (b j e) -> p b j e", b=2, j=GROUP)
        copies = sb("copies", [P, 2, GROUP])
        keep = sb("keep", [P, 2, GROUP])
        scatter_idx = sb("scatter_idx", [P, 2, GROUP], I32)
        sums = gathered

        pst = ctx.enter_context(nc.psum_tensor("pst", [P, 8, BANK], F32))

        SUMS, LOOK, TURNED, COEF, PRODUCT = 0, 1, 2, 3, 4

        copied = [sem(f"copied{b}") for b in range(2)]
        spare_filled = sem("spare_filled")
        tables_loaded = sem("tables_loaded")
        padded = sem("padded")
        weights_loaded = sem("weights_loaded")
        iota_ready = sem("iota_ready")
        ident_ready = sem("ident_ready")
        ident_cleared = sem("ident_cleared")
        dve_step = sem("dve_step")
        table_float = sem("table_float")
        table_turned = sem("table_turned")
        idx_ready = sem("idx_ready")
        hot_ready = sem("hot_ready")
        hot_used = sem("hot_used")
        degree_copied = sem("degree_copied")
        degree_turned_ps = sem("degree_turned_ps")
        degree_ready = sem("degree_ready")
        table_clamped = sem("table_clamped")
        table_root = sem("table_root")
        table_ready = sem("table_ready")
        inverse_ready = sem("inverse_ready")
        table_stored = sem("table_stored")
        row_table_ready = sem("row_table_ready")
        rows_stored = sem("rows_stored")
        edge_row_loaded = [sem(f"edge_row_loaded{b}") for b in range(2)]
        turned_hot_ready = sem("turned_hot_ready")
        look_ps = sem("look_ps")
        picked_ready = sem("picked_ready")
        degree_kept = sem("degree_kept")
        coef_kept = sem("coef_kept")
        idx_staged = sem("idx_staged")
        row_gathered = [sem(f"row_gathered{b}") for b in range(2)]
        look_staged = sem("look_staged")
        look_done = [sem(f"look_done{b}") for b in range(2)]
        src_norm_ready = sem("src_norm_ready")
        row_summed = sem("row_summed")
        mean_ready = sem("mean_ready")
        row_squared = sem("row_squared")
        squares_kept = sem("squares_kept")
        act_turn = sem("act_turn")
        root_in = sem("root_in")
        root_done = sem("root_done")
        norm_ready = sem("norm_ready")
        h_ready = sem("h_ready")
        h_turned_ps = sem("h_turned_ps")
        h_turned_ready = sem("h_turned_ready")
        product_ready = sem("product_ready")
        first_part = sem("first_part")
        second_part = sem("second_part")
        third_part = sem("third_part")
        message_ready = sem("message_ready")
        src_row_loaded = [sem(f"src_row_loaded{b}") for b in range(2)]
        same_ready = sem("same_ready")
        keep_ready = sem("keep_ready")
        scatter_idx_ready = sem("scatter_idx_ready")
        sums_ps = sem("sums_ps")
        sums_ready = sem("sums_ready")
        scattered = sem("scattered")
        pool_turn = sem("pool_turn")

        def groups(body, eng, first=0, end=GROUPS):
            i = first
            while i < 2:
                body(i, i % 2)
                i += 1
            loop_end = min(end, GROUPS - 3)
            if loop_end > i:
                assert i % 2 == 0 and (loop_end - i) % 2 == 0
                with eng.Fori(i, loop_end - 1, 2) as k:
                    body(k, 0)
                    body(k + 1, 1)
                i = loop_end
            for j in range(i, end):
                body(j, j % 2)

        block = ctx.enter_context(nc.Block())

        @block.sync
        def _(sp):
            def load_table(slot, array):
                sp.dma_start(table_i[:, slot, :], array[0:HALF * P].rearrange("(t p) -> t p", p=P)) \
                    .then_inc(tables_loaded, 16)
                full = (HALF + LAST_ROWS) * P
                sp.dma_start(table_i[0:LAST_ROWS, slot + 1, :],
                             array[HALF * P:full].rearrange("(t p) -> t p", p=P)).then_inc(tables_loaded, 16)
                sp.dma_start(table_i[LAST_ROWS:LAST_ROWS + 1, slot + 1, 0:LAST_EDGES],
                             array[full:E].rearrange("(t p) -> t p", t=1)).then_inc(tables_loaded, 16)

            sp.wait_ge(padded, 4)
            load_table(0, dst)
            load_table(2, src)
            load_table(4, edge_type)
            sp.dma_start(comps_sb[:], comps).then_inc(weights_loaded, 16)
            sp.dma_start(alpha_sb[:], alpha).then_inc(weights_loaded, 16)
            sp.dma_start(bases_sb[:], bases.rearrange("b d f -> d b f")).then_inc(weights_loaded, 16)
            extra = out.shape[0] - N
            sp.dma_start(out[N:N + extra, :], x[0:extra, :]).then_inc(spare_filled, 16)
            sp.wait_ge(row_table_ready, 2)
            for k in range(2):
                sp.dma_start(edge_row_dram[k, :].rearrange("(h t p) -> t h p", h=2, p=P),
                             table_row[:, 2 * k:2 * k + 2, :]).then_inc(rows_stored, 16)

            def copy(i, b):
                if not (isinstance(i, int) and i < 2):
                    sp.wait_ge(copied[b], (i - b) * 8)
                a = i * COPY_ROWS
                flat_out, flat_x = (y[bass.ds(a, COPY_ROWS), :].rearrange("r d -> (r d)") for y in (out, x))
                sp.dma_start(flat_out.rearrange("(q e) -> q e", q=16), flat_x.rearrange("(q e) -> q e", q=16)) \
                    .then_inc(copied[b], 16)

            copy(0, 0)
            copy(1, 1)
            with sp.Fori(2, EARLY_COPIES - 1, 2) as k:
                copy(k, 0)
                copy(k + 1, 1)
            sp.wait_ge(rows_stored, 32)

            def load_edge_row(i, b):
                if not (isinstance(i, int) and i < 2):
                    sp.wait_ge(turned_hot_ready, i - 1)
                sp.dma_start(edge_row[:, b, :, :],
                             edge_row_dram[:, bass.ds(i * W, W)].rearrange("(o k) e -> o k e", o=1)
                             .to_broadcast([P, 2, W])).then_inc(edge_row_loaded[b], 16)

            load_edge_row(0, 0)
            load_edge_row(1, 1)
            with sp.Fori(1, AHEAD // 2) as k:
                load_edge_row(2 * k, 0)
                load_edge_row(2 * k + 1, 1)
                for c in range(4):
                    copy(EARLY_COPIES + 4 * (k - 1) + c, c % 2)

            def load_src_row(i, b):
                last = isinstance(i, int) and i == GROUPS - 1
                if not (isinstance(i, int) and i < 2):
                    sp.wait_ge(same_ready, GROUP * (i - 1))
                n = LAST_GROUP if last else GROUP * P
                sp.dma_start(src_row[:, b, 0:n],
                             src[bass.ds(i * (GROUP * P), n)].rearrange("(o e) -> o e", o=1).to_broadcast([P, n])) \
                    .then_inc(src_row_loaded[b], 16)

            def load_rows(i, b):
                load_src_row(i, b)
                load_edge_row(i + AHEAD, b)

            groups(load_rows, sp, 0, GROUPS - 1 - AHEAD)
            load_rows(GROUPS - 1 - AHEAD, 0)
            load_src_row(GROUPS - AHEAD, 1)
            groups(load_src_row, sp, GROUPS - AHEAD + 1, GROUPS)
            sp.wait_ge(spare_filled, 16)
            for b in range(2):
                sp.wait_ge(copied[b], 8 * COPIES)
            sp.wait_ge(rows_stored, 32)
            sp.wait_ge(table_stored, 16)
            sp.wait_ge(scattered, 16 * TILES)

        @block.gpsimd
        def _(pool):
            pool.iota(iota_i[:], [[1, HI]], base=0, channel_multiplier=0).then_inc(iota_ready, 1)
            pool.iota(chunk_id_i[:], [[CH, CHUNKS]], base=0, channel_multiplier=1).then_inc(iota_ready, 1)
            pool.iota(spare_i[:], [[P, GROUP]], base=SPARE, channel_multiplier=1).then_inc(iota_ready, 1)
            pool.memset(ident[:], 0.0).then_inc(ident_cleared, 1)
            pool.memset(later[:], 1.0).then_inc(ident_cleared, 1)
            pool.wait_ge(ident_cleared, 2)
            pool.affine_select(out=ident[:], in_=ident[:], compare_op=ALU.not_equal, fill=1.0, base=0,
                               pattern=[[-1, P]], channel_multiplier=1).then_inc(ident_ready, 1)
            pool.affine_select(out=later[:, 0:P], in_=later[:, 0:P], compare_op=ALU.is_ge, fill=0.0, base=0,
                               pattern=[[1, P]], channel_multiplier=-1).then_inc(ident_ready, 1)

            def gather_rows(i, b):
                if not (isinstance(i, int) and i < 2):
                    pool.wait_ge(row_summed, i - 1)
                pool.wait_ge(idx_staged, i + 1)
                pool.sem_inc(pool_turn)
                for j in range(GROUP):
                    pool.indirect_dma_start(gathered[:, b, j, :], None, x,
                                            bass.IndirectOffsetOnAxis(ap=gather_idx[:, b, j:j + 1], axis=0)) \
                        .then_inc(row_gathered[b], 16)

            groups(gather_rows, pool)

            pool.wait_ge(table_stored, 16)
            pool.wait_ge(idx_ready, 2)

            def keep_looked(i, b):
                pool.wait_ge(look_done[b], (i - b) * (8 * GROUP) + 16 * GROUP)
                pool.tensor_copy(src_norm[:, bass.ds(i * GROUP, GROUP)], looked[:, b, :]).then_inc(src_norm_ready, 1)

            def stage_look(i, b):
                if not (isinstance(i, int) and i < 2):
                    keep_looked(i - 2, b)
                pool.tensor_copy(look_idx[:, b, :], src_i[:, bass.ds(i * GROUP, GROUP)]).then_inc(look_staged, 1)
                if not (isinstance(i, int) and i < 2):
                    pool.wait_ge(src_norm_ready, i - 1)
                pool.wait_ge(look_staged, i + 1)
                pool.sem_inc(pool_turn)

            def look_up_tiles(b, tiles):
                for j in tiles:
                    pool.indirect_dma_start(looked[:, b, j:j + 1], None, inverse_root_dram,
                                            bass.IndirectOffsetOnAxis(ap=look_idx[:, b, j:j + 1], axis=0)) \
                        .then_inc(look_done[b], 16)

            def look_up(i, b):
                stage_look(i, b)
                look_up_tiles(b, range(GROUP))

            def scatter(i, b):
                pool.wait_ge(scatter_idx_ready, i + 1)
                pool.wait_ge(sums_ready, GROUP * (i + 1))
                if not (isinstance(i, int) and i == 0):
                    pool.wait_ge(scattered, 16 * GROUP * i)
                pool.sem_inc(pool_turn)
                for j in range(GROUP):
                    pool.indirect_dma_start(out, bass.IndirectOffsetOnAxis(ap=scatter_idx[:, b, j:j + 1], axis=0),
                                            sums[:, b, j, :], None, bounds_check=out.shape[0] - 1,
                                            oob_is_err=True, compute_op=ALU.add).then_inc(scattered, 16)

            groups(look_up, pool, 0, LEAD)
            pool.wait_ge(spare_filled, 16)
            for b in range(2):
                pool.wait_ge(copied[b], 8 * COPIES)

            def four_scatters(k):
                i, n = 4 * k, LEAD + 6 * k
                scatter(i, 0)
                look_up(n, 0)
                look_up(n + 1, 1)
                scatter(i + 1, 1)
                look_up(n + 2, 0)
                scatter(i + 2, 0)
                look_up(n + 3, 1)
                look_up(n + 4, 0)
                scatter(i + 3, 1)
                look_up(n + 5, 1)

            four_scatters(0)
            with pool.Fori(1, QUICK) as k:
                four_scatters(k)

            with pool.Fori(4 * QUICK, SPARSE_AT - 1, 2) as k:
                for b in range(2):
                    scatter(k + b, b)
                    look_up(k + b + LEAD + 2 * QUICK, b)

            with pool.Fori(0, SPARSE) as k:
                for b in range(2):
                    for half in range(2):
                        scatter(SPARSE_AT + 4 * k + 2 * b + half, half)
                        if half == 0:
                            stage_look(SPARSE_AT + LEAD + 2 * QUICK + 2 * k + b, b)
                        look_up_tiles(b, range(half * GROUP // 2, (half + 1) * GROUP // 2))

            scatter(ALONE_AT, 0)
            look_up(GROUPS - 1, 0)
            scatter(ALONE_AT + 1, 1)
            keep_looked(GROUPS - 2, 1)
            keep_looked(GROUPS - 1, 0)
            for i in range(ALONE_AT + 2, GROUPS):
                scatter(i, i % 2)

        @block.vector
        def _(dve):
            steps = [0]

            def step(ins):
                steps[0] += 1
                ins.then_inc(dve_step, 1)
                dve.wait_ge(dve_step, steps[0])

            dve.memset(table_i[:, 1, :], 0).then_inc(padded, 1)
            dve.memset(table_i[:, 3, :], PAD_NODE).then_inc(padded, 1)
            dve.memset(table_i[:, 5, :], 0).then_inc(padded, 1)
            dve.memset(eps[:], EPS).then_inc(padded, 1)
            dve.wait_ge(iota_ready, 3)
            dve.tensor_copy(iota_h[:], iota_i[:])
            dve.tensor_copy(chunk_id[:], chunk_id_i[:])
            step(dve.tensor_copy(spare[:], spare_i[:]))
            dve.wait_ge(tables_loaded, 16 * 9)
            dve.tensor_copy(table_f[:], table_i[:, 0:4, :]).then_inc(table_float, 1)
            step(dve.tensor_scalar(table_hi[:], table_i[:, 0:2, :], P.bit_length() - 1, None,
                                   ALU.logical_shift_right))
            dve.tensor_copy(table_row[:, 0:2, :], table_hi[:]).then_inc(row_table_ready, 1)
            dve.tensor_copy(table_row[:, 2:4, :], table_i[:, 4:6, :]).then_inc(row_table_ready, 1)
            dve.wait_ge(table_turned, 1)
            turned = pst[:, 2, 0:4 * HALF].rearrange("p (k t) -> p k t", k=4)
            dve.tensor_copy(dst_i[:].rearrange("p (k t) -> p k t", k=2), turned[:, 0:2, :]).then_inc(idx_ready, 1)
            dve.wait_ge(idx_ready, 1)
            step(dve.tensor_copy(src_i[:].rearrange("p (k t) -> p k t", k=2), turned[:, 2:4, :]))
            step(dve.tensor_copy(src_f[:].rearrange("p (k t) -> p k t", k=2), turned[:, 2:4, :]))
            step(dve.tensor_scalar(part_i[:, 0, :], src_i[:], HIST_LO.bit_length() - 1, None, ALU.logical_shift_right))
            step(dve.tensor_scalar(part_i[:, 1, :], src_i[:], HIST_LO - 1, None, ALU.bitwise_and))
            step(dve.tensor_scalar(part_i[:, 2, :], dst_i[:], P - 1, None, ALU.bitwise_and))
            dve.tensor_copy(hi_f[:], part_i[:, 0, :])
            dve.tensor_copy(dst_lo_f[:], part_i[:, 2, :])
            step(dve.tensor_copy(lo_f[:], part_i[:, 1, :]))
            step(dve.tensor_tensor(src_less_spare[:].rearrange("p (g j) -> p g j", j=GROUP),
                                   src_f[:].rearrange("p (g j) -> p g j", j=GROUP),
                                   spare[:].rearrange("p (g j) -> p g j", g=1).to_broadcast([P, GROUPS, GROUP]),
                                   ALU.subtract))
            dve.nop().then_inc(idx_ready, 1)

            def hots(i, b):
                if not (isinstance(i, int) and i < 2):
                    dve.wait_ge(hot_used, GROUP * (i - 1))
                for j in range(GROUP):
                    t = i * GROUP + j
                    dve.tensor_scalar(lo_hot[:, b, j, :], iota_h[:, 0:HIST_LO], lo_f[:, bass.ds(t, 1)], None,
                                      ALU.is_equal)
                    dve.tensor_scalar(hi_hot[:, b, j, :], iota_h[:, 0:HIST_HI], hi_f[:, bass.ds(t, 1)], None,
                                      ALU.is_equal).then_inc(hot_ready, 1)

            groups(hots, dve)
            dve.wait_ge(hot_used, TILES)
            for k in range(LO_TILES):
                dve.tensor_copy(degree[:].rearrange("p (h k) -> p k h", k=LO_TILES)[:, k, :], pst[:, k, 0:HIST_HI]) \
                    .then_inc(degree_copied, 1)
            for c in range(CHUNKS):
                dve.wait_ge(degree_turned_ps, min(c - c % 4 + 4, CHUNKS))
                dve.tensor_copy(degree_turned[:, c, :], pst[0:CH, 3 + c // 4, (c % 4) * P:(c % 4 + 1) * P]) \
                    .then_inc(degree_ready, 1)

            dve.wait_ge(degree_ready, CHUNKS)
            dve.tensor_scalar(inverse_root[:], degree_turned[:], 1.0, None, ALU.max).then_inc(table_clamped, 1)
            step(dve.tensor_copy(degree_i[:], degree_turned[:]))
            step(dve.tensor_scalar(degree_i[:], degree_i[:], LOW - 1, None, ALU.bitwise_and))
            step(dve.tensor_copy(degree_parts[:, 0, :, :], degree_i[:]))
            step(dve.tensor_tensor(degree_parts[:, 1, :, :], degree_turned[:], degree_parts[:, 0, :, :],
                                   ALU.subtract))
            dve.wait_ge(weights_loaded, 16 * 3)
            step(dve.tensor_scalar(comps_rest[:], comps_sb[:], alpha_sb[:, 0:1], None, ALU.mult))
            for k in range(SPLITS):
                step(dve.tensor_copy(comps_split[:, k, :], comps_rest[:]))
                if k < SPLITS - 1:
                    step(dve.tensor_tensor(comps_rest[:], comps_rest[:], comps_split[:, k, :], ALU.subtract))
            dve.nop().then_inc(table_ready, 1)

            def turned_hots(i, b):
                dve.wait_ge(edge_row_loaded[b], (i - b) * 8 + 16)
                if not (isinstance(i, int) and i < 2):
                    dve.wait_ge(look_ps, i - 1)
                for c in range(CHUNKS):
                    dve.tensor_scalar(node_hot[0:CH, b, c, :], edge_row[0:CH, b, 0, :], chunk_id[0:CH, c:c + 1], None,
                                      ALU.is_equal)
                dve.tensor_scalar(type_hot[0:R, b, :], edge_row[0:R, b, 1, :], chunk_id[0:R, 0:1], None,
                                  ALU.is_equal).then_inc(turned_hot_ready, 1)

            def pick(i, b, bank=0):
                dve.wait_ge(look_ps, i + 1)
                if not (isinstance(i, int) and i < 2):
                    dve.wait_ge(degree_kept, i - 1)
                for j in range(GROUP):
                    dve.scalar_tensor_tensor(out=masked[:, j, :], in0=iota_h[:, 0:P],
                                             scalar=dst_lo_f[:, bass.ds(i * GROUP + j, 1)],
                                             in1=pst[:, LOOK + bank, j * P:(j + 1) * P], op0=ALU.is_equal, op1=ALU.mult,
                                             accum_out=picked[:, b, j:j + 1]).then_inc(picked_ready, 1)

            def keep_picked(i, b):
                dve.tensor_copy(coef[:, bass.ds(i * GROUP, GROUP), :].rearrange("p t b -> p (t b)"),
                                pst[:, COEF + b, 0:GROUP * B]).then_inc(coef_kept, 1)
                dve.wait_ge(picked_ready, GROUP * (i + 1))
                dve.tensor_copy(dst_degree[:, bass.ds(i * GROUP, GROUP)], picked[:, b, :]).then_inc(degree_kept, 1)

            def look(i, b):
                turned_hots(i, b)
                if not (isinstance(i, int) and i < 1):
                    pick(i - 1, 1 - b, 1 - b)
                    keep_picked(i - 1, 1 - b)

            groups(look, dve, 0, INVERT_AT)
            dve.wait_ge(table_root, 1)
            step(dve.reciprocal(inverse_root[:], inverse_root[:]))
            dve.scalar_tensor_tensor(out=inverse_root[:], in0=degree_turned[:], scalar=1.0, in1=inverse_root[:],
                                     op0=ALU.min, op1=ALU.mult).then_inc(inverse_ready, 1)
            groups(look, dve, INVERT_AT, AHEAD)
            pick(AHEAD - 1, 1, 1)
            keep_picked(AHEAD - 1, 1)

            def norms(first, end, roots):
                t = slice(first * GROUP, end * GROUP)
                dve.wait_ge(degree_kept, end)
                dve.wait_ge(coef_kept, end)
                dve.tensor_scalar(dst_root[:, t], dst_degree[:, t], 1.0, None, ALU.max).then_inc(root_in, 1)
                dve.wait_ge(root_done, roots + 1)
                step(dve.reciprocal(rstd[:, t], rstd[:, t]))
                step(dve.tensor_tensor(shift[:, t], shift[:, t], rstd[:, t], ALU.mult))
                dve.wait_ge(root_done, roots + 2)
                step(dve.reciprocal(dst_root[:, t], dst_root[:, t]))
                step(dve.scalar_tensor_tensor(out=dst_root[:, t], in0=dst_degree[:, t], scalar=1.0,
                                              in1=dst_root[:, t], op0=ALU.min, op1=ALU.mult))
                dve.tensor_tensor(coef[:, t, :], coef[:, t, :],
                                  dst_root[:, t].rearrange("p (t o) -> p t o", o=1)
                                  .to_broadcast([P, (end - first) * GROUP, B]), ALU.mult).then_inc(norm_ready, 1)

            norms(0, AHEAD, 0)

            def messages(i, b):
                def add(j, term, before, after, out=None):
                    t = i * GROUP + j
                    u = pst[:, PRODUCT + j, term * D:(term + 1) * D]
                    c = coef[:, bass.ds(t, 1), :].rearrange("p a b -> p (a b)")
                    dve.wait_ge(before, t + 1)
                    dve.scalar_tensor_tensor(out=part_sum[:, b, j, :] if out is None else out, in0=u,
                                             scalar=c[:, term:term + 1], in1=part_sum[:, b, j, :],
                                             op0=ALU.mult, op1=ALU.add).then_inc(after, 1)

                for pair in range(0, GROUP, 2):
                    for j in (pair, pair + 1):
                        add(j, 1, first_part, second_part)
                    for j in (pair, pair + 1):
                        add(j, 2, second_part, third_part)
                    for j in (pair, pair + 1):
                        add(j, 3, third_part, message_ready,
                            rows[:, bass.ds(i * GROUP + j, 1), :].rearrange("p a d -> p (a d)"))

            def same_src(i, b):
                if isinstance(i, int) and i == GROUPS - 1:
                    dve.wait_ge(same_ready, GROUP * (GROUPS - 2))
                    dve.memset(src_row[:, b, LAST_GROUP:], PAD_NODE).then_inc(padded, 1)
                    dve.wait_ge(padded, 5)
                dve.wait_ge(src_row_loaded[b], 16 * ((i - b) // 2 + 1) if isinstance(i, int) else
                            (i - b) * 8 + 16)
                if not (isinstance(i, int) and i < 2):
                    dve.wait_ge(sums_ps, i - 1)
                    dve.wait_ge(scattered, 16 * GROUP * (i - 1))
                for j in range(GROUP):
                    t = i * GROUP + j
                    w = (GROUP - j) * P
                    dve.scalar_tensor_tensor(out=same[:, b, j, 0:w], in0=src_row[:, b, j * P:],
                                             scalar=src_f[:, bass.ds(t, 1)], in1=later[:, 0:w],
                                             op0=ALU.is_equal, op1=ALU.mult,
                                             accum_out=copies[:, b, j:j + 1]).then_inc(same_ready, 1)
                dve.wait_ge(same_ready, GROUP * (i + 1))
                dve.scalar_tensor_tensor(out=keep[:, b, :], in0=copies[:, b, :], scalar=1.0,
                                         in1=src_less_spare[:, bass.ds(i * GROUP, GROUP)], op0=ALU.is_equal,
                                         op1=ALU.mult).then_inc(keep_ready, 1)
                dve.wait_ge(keep_ready, i + 1)
                dve.tensor_tensor(scatter_idx[:, b, :], keep[:, b, :], spare[:], ALU.add) \
                    .then_inc(scatter_idx_ready, 1)

            def messages_and_same(i, b):
                messages(i, b)
                same_src(i, b)

            def with_look(i, b):
                turned_hots(i + AHEAD, b)
                messages(i, b)
                same_src(i, b)
                pick(i + AHEAD, b)

            groups(with_look, dve, 0, GROUPS - 1 - AHEAD)
            with_look(GROUPS - 1 - AHEAD, 0)
            norms(AHEAD, GROUPS, 2)
            messages_and_same(GROUPS - AHEAD, 1)
            groups(messages_and_same, dve, GROUPS - AHEAD + 1, GROUPS)

        @block.scalar
        def _(act):
            def stage_idx(i, b):
                act.activation(gather_idx[:, b, :], dst_i[:, bass.ds(i * GROUP, GROUP)], ACT.Copy) \
                    .then_inc(idx_staged, 1)

            def keep_rows(i, b):
                act.wait_ge(row_gathered[b], (i - b) * (8 * GROUP) + 16 * GROUP)
                if not (isinstance(i, int) and i + 2 >= GROUPS):
                    stage_idx(i + 2, b)
                for j in range(GROUP):
                    last = act.activation(rows[:, bass.ds(i * GROUP + j, 1), :].rearrange("p a d -> p (a d)"),
                                          gathered[:, b, j, :], ACT.Copy, accum_out=row_sum[:, b, j:j + 1])
                last.then_inc(row_summed, 1)
                act.wait_ge(row_summed, i + 1)
                act.activation(mean[:, b, :], row_sum[:, b, :], ACT.Copy, scale=-1.0 / D) \
                    .then_inc(mean_ready, 1)
                act.wait_ge(mean_ready, i + 1)
                act.sem_inc(act_turn)
                for j in range(GROUP):
                    last = act.activation(squared[:, j, :], rows[:, bass.ds(i * GROUP + j, 1), :]
                                          .rearrange("p a d -> p (a d)"), ACT.Square,
                                          bias=mean[:, b, j:j + 1],
                                          accum_out=row_squares[:, b, j:j + 1])
                last.then_inc(row_squared, 1)
                act.wait_ge(row_squared, i + 1)
                act.sem_inc(act_turn)
                act.activation(shift[:, bass.ds(i * GROUP, GROUP)], mean[:, b, :], ACT.Copy)
                act.activation(squares[:, bass.ds(i * GROUP, GROUP)], row_squares[:, b, :], ACT.Copy) \
                    .then_inc(squares_kept, 1)

            act.wait_ge(idx_ready, 1)
            stage_idx(0, 0)
            stage_idx(1, 1)
            groups(keep_rows, act, 0, ROOT_AT)
            act.wait_ge(table_clamped, 1)
            act.activation(inverse_root[:], inverse_root[:], ACT.Sqrt).then_inc(table_root, 1)
            groups(keep_rows, act, ROOT_AT, STORE_AT)
            act.wait_ge(inverse_ready, 1)
            act.dma_start(inverse_root_dram.rearrange("(c r l) o -> r c (l o)", c=CHUNKS, l=P), inverse_root[:]) \
                .then_inc(table_stored, 16)
            groups(keep_rows, act, STORE_AT, GROUPS)

            def roots(first, end, before):
                t = slice(first * GROUP, end * GROUP)
                act.wait_ge(squares_kept, GROUPS)
                act.activation(rstd[:, t], squares[:, t], ACT.Sqrt, bias=eps[:, 0:1], scale=1.0 / D) \
                    .then_inc(root_done, 1)
                act.wait_ge(root_in, before + 1)
                act.activation(dst_root[:, t], dst_root[:, t], ACT.Sqrt).then_inc(root_done, 1)

            roots(0, AHEAD, 0)

            def relu(i, b):
                if not (isinstance(i, int) and i < 2):
                    act.wait_ge(h_turned_ps, i - 1)
                for j in range(GROUP):
                    t = i * GROUP + j
                    last = act.activation(h[:, b, j, :], rows[:, bass.ds(t, 1), :].rearrange("p a d -> p (a d)"),
                                          ACT.Relu, bias=shift[:, bass.ds(t, 1)], scale=rstd[:, bass.ds(t, 1)])
                last.then_inc(h_ready, 1)

            def keep_turned(i, b):
                act.wait_ge(h_turned_ps, i + 1)
                if not (isinstance(i, int) and i < 2):
                    act.wait_ge(product_ready, GROUP * (i - 1))
                act.activation(h_turned[:, b, :, :].rearrange("p t e -> p (t e)"), pst[:, TURNED, :], ACT.Copy) \
                    .then_inc(h_turned_ready, 1)

            def first(i, b, j):
                t = i * GROUP + j
                act.wait_ge(product_ready, t + 1)
                if not (isinstance(i, int) and i < 2):
                    act.wait_ge(message_ready, GROUP * (i - 1))
                act.activation(part_sum[:, b, j, :], pst[:, PRODUCT + j, 0:D], ACT.Copy,
                               scale=coef[:, bass.ds(t, 1), :].rearrange("p a b -> p (a b)")[:, 0:1]) \
                    .then_inc(first_part, 1)

            act.wait_ge(norm_ready, 1)
            relu(0, 0)
            relu(1, 1)
            keep_turned(0, 0)

            def transform(i, b):
                first(i, b, 0)
                first(i, b, 1)
                if not (isinstance(i, int) and i + 1 >= GROUPS):
                    keep_turned(i + 1, 1 - b)
                if not (isinstance(i, int) and i + 2 >= GROUPS):
                    relu(i + 2, b)
                first(i, b, 2)
                first(i, b, 3)

            def scale_sums(i, b):
                act.wait_ge(sums_ps, i + 1)
                act.wait_ge(src_norm_ready, i + 1)
                if not (isinstance(i, int) and i < 2):
                    act.wait_ge(scattered, 16 * GROUP * (i - 1))
                for j in range(GROUP):
                    act.activation(sums[:, b, j, :], pst[:, SUMS, j * P:(j + 1) * P], ACT.Copy,
                                   scale=src_norm[:, bass.ds(i * GROUP + j, 1)]).then_inc(sums_ready, 1)

            def transform_and_scale(i, b):
                transform(i, b)
                if not (isinstance(i, int) and i < 1):
                    scale_sums(i - 1, 1 - b)

            def keep_picked(i, b):
                act.wait_ge(look_ps, i + 1)
                act.activation(coef[:, bass.ds(i * GROUP, GROUP), :].rearrange("p t b -> p (t b)"),
                               pst[:, COEF, 0:GROUP * B], ACT.Copy).then_inc(coef_kept, 1)
                act.wait_ge(picked_ready, GROUP * (i + 1))
                act.activation(dst_degree[:, bass.ds(i * GROUP, GROUP)], picked[:, b, :], ACT.Copy) \
                    .then_inc(degree_kept, 1)

            def with_look(i, b):
                transform_and_scale(i, b)
                keep_picked(i + AHEAD, b)

            groups(with_look, act, 0, GROUPS - 1 - AHEAD)
            with_look(GROUPS - 1 - AHEAD, 0)
            roots(AHEAD, GROUPS, 1)
            act.wait_ge(norm_ready, 2)
            transform_and_scale(GROUPS - AHEAD, 1)
            groups(transform_and_scale, act, GROUPS - AHEAD + 1, GROUPS)
            scale_sums(GROUPS - 1, 0)

        @block.tensor
        def _(pe):
            pe.wait_ge(ident_ready, 2)
            pe.wait_ge(table_float, 1)
            for k in range(4):
                last = pe.transpose(pst[:, 2, k * HALF:(k + 1) * HALF], table_f[:, k, :], ident[0:HALF, 0:HALF])
            last.then_inc(table_turned, 1)

            def histogram(i, b):
                for j in range(GROUP):
                    t = i * GROUP + j
                    start = isinstance(i, int) and i == 0 and j == 0
                    stop = isinstance(i, int) and i == GROUPS - 1 and j == GROUP - 1
                    pe.wait_ge(hot_ready, t + 1)
                    for k in range(LO_TILES):
                        last = pe.matmul(pst[:, k, 0:HIST_HI], lo_hot[:, b, j, k * P:(k + 1) * P], hi_hot[:, b, j, :],
                                         start=start, stop=stop)
                    last.then_inc(hot_used, 1)

            groups(histogram, pe)
            pe.wait_ge(degree_copied, LO_TILES)
            for c in range(CHUNKS):
                pe.transpose(pst[0:CH, 3 + c // 4, (c % 4) * P:(c % 4 + 1) * P], degree[:, c * CH:(c + 1) * CH],
                             ident[:]).then_inc(degree_turned_ps, 1)

            pe.wait_ge(table_ready, 1)

            def look(i, b, bank, since):
                pe.wait_ge(turned_hot_ready, i + 1)
                if not (isinstance(i, int) and i < since):
                    pe.wait_ge(picked_ready, GROUP * (i - since + 1))
                    pe.wait_ge(coef_kept, i - since + 1)
                for j in range(GROUP):
                    for c in range(CHUNKS):
                        for k in range(PARTS):
                            pe.matmul(pst[:, LOOK + bank, j * P:(j + 1) * P], node_hot[0:CH, b, c, j * P:(j + 1) * P],
                                      degree_parts[:, k, c, :], start=(c == 0 and k == 0),
                                      stop=(c == CHUNKS - 1 and k == PARTS - 1))
                    for k in range(SPLITS):
                        last = pe.matmul(pst[:, COEF + bank, j * B:(j + 1) * B], type_hot[0:R, b, j * P:(j + 1) * P],
                                         comps_split[:, k, :], start=(k == 0), stop=(k == SPLITS - 1))
                last.then_inc(look_ps, 1)

            groups(lambda i, b: look(i, b, b, 2), pe, 0, AHEAD)

            def turn(i, b):
                pe.wait_ge(h_ready, i + 1)
                if not (isinstance(i, int) and i < 1):
                    pe.wait_ge(h_turned_ready, i)
                for j in range(GROUP):
                    last = pe.transpose(pst[:, TURNED, j * P:(j + 1) * P], h[:, b, j, :], ident[:])
                last.then_inc(h_turned_ps, 1)

            def multiply(i, b):
                pe.wait_ge(h_turned_ready, i + 1)
                for j in range(GROUP):
                    if not (isinstance(i, int) and i < 1):
                        pe.wait_ge(message_ready, (i - 1) * GROUP + j + 1)
                    pe.matmul(pst[:, PRODUCT + j, :], h_turned[:, b, j, :], bases_sb[:].rearrange("d b f -> d (b f)"),
                              start=True, stop=True).then_inc(product_ready, 1)

            def add_same(i, b):
                pe.wait_ge(same_ready, GROUP * (i + 1))
                pe.wait_ge(message_ready, GROUP * (i + 1))
                if not (isinstance(i, int) and i < 1):
                    pe.wait_ge(sums_ready, GROUP * i)
                for t in range(GROUP):
                    for s in range(t + 1):
                        last = pe.matmul(pst[:, SUMS, t * P:(t + 1) * P], same[:, b, s, (t - s) * P:(t - s + 1) * P],
                                         rows[:, bass.ds(i * GROUP + s, 1), :].rearrange("p a d -> p (a d)"),
                                         start=(s == 0), stop=(s == t))
                last.then_inc(sums_ps, 1)

            def multiply_and_add(i, b):
                if not (isinstance(i, int) and i + 1 >= GROUPS):
                    turn(i + 1, 1 - b)
                multiply(i, b)
                if not (isinstance(i, int) and i < 1):
                    add_same(i - 1, 1 - b)

            def with_look(i, b):
                turn(i + 1, 1 - b)
                multiply(i, b)
                if not (isinstance(i, int) and i < 1):
                    add_same(i - 1, 1 - b)
                look(i + AHEAD, b, 0, 1)

            turn(0, 0)
            groups(with_look, pe, 0, GROUPS - 1 - AHEAD)
            with_look(GROUPS - 1 - AHEAD, 0)
            multiply_and_add(GROUPS - AHEAD, 1)
            groups(multiply_and_add, pe, GROUPS - AHEAD + 1, GROUPS)
            add_same(GROUPS - 1, 0)


_INS = ['x', 'src', 'dst', 'edge_type_50', 'L0_gnn_bases', 'L0_gnn_comps', 'L0_gnn_alpha']


def kernel(**inputs):
    import numpy as _np
    import concourse.bacc as _bacc
    from concourse import mybir as _mybir
    from concourse.bass_utils import run_bass_kernel_spmd as _run

    nc = _bacc.Bacc("TRN2", target_bir_lowering=False, num_devices=1)
    arrays, args = {}, []
    for name in _INS:
        a = _np.ascontiguousarray(inputs[name])
        arrays[f"in_{name}_dram"] = a
        args.append(nc.dram_tensor(f"in_{name}_dram", a.shape, _mybir.dt.from_np(a.dtype), kind="ExternalInput").ap())
    nodes, width = inputs["x"].shape
    args.append(nc.dram_tensor("out_dram", (padded_rows(nodes), width), _mybir.dt.float32,
                               kind="ExternalOutput").ap())
    build(nc, *args)
    r = _run(nc, [arrays], core_ids=[0])
    return r.results[0]["out_dram"][:nodes]
```

```python
from contextlib import ExitStack

import concourse.bass as bass
from concourse import mybir

ALU = mybir.AluOpType
ACT = mybir.ActivationFunctionType
F32 = mybir.dt.float32
F16 = mybir.dt.float16
BF16 = mybir.dt.bfloat16
I32 = mybir.dt.int32

P = 128
GROUP = 4
EPS = 1e-5


def padded_rows(nodes):
    return -(-(nodes + GROUP * P + 1) // P) * P


def build(nc, x, src, dst, edge_type, bases, comps, alpha, out):
    N, D = x.shape
    E = src.shape[0]
    R, B = comps.shape
    TILES = -(-E // P)
    GROUPS = TILES // GROUP
    HALF = TILES // 2
    assert D == P and TILES == GROUPS * GROUP and TILES == 2 * HALF and HALF <= P and GROUPS % 2 == 1
    LAST_ROWS = E // P - HALF
    LAST_EDGES = E % P
    LAST_GROUP = E - (GROUPS - 1) * GROUP * P
    SPARE = N
    PAD_NODE = N + GROUP * P
    CHUNKS = 7
    CH = -(-(PAD_NODE // P + 1) // CHUNKS)
    CH += CH % 2
    HI = CHUNKS * CH
    BANK = 512
    PARTS = 2
    LOW = 2048
    SPLITS = 3
    COPIES = 2 * (GROUPS + 1)
    COPY_ROWS = N // COPIES
    RING = 4
    AHEAD = 28
    OWN = 4
    SLOTS = OWN + GROUPS
    LATE = 24
    EARLY_COPIES = COPIES - 2 * LATE
    assert OWN % RING == AHEAD % RING == LATE % RING == (GROUPS - 1) % RING == 0 and 0 < LATE < AHEAD
    assert 0 < OWN * GROUP <= HALF and AHEAD > GROUPS - AHEAD + 1
    ROOT_AT, STORE_AT = 24, 34
    LEAD, QUICK, EVEN = 10, 2, 10
    SPARSE = (GROUPS - OWN - 1 - LEAD - 6 * QUICK - EVEN) // 2
    SPARSE_AT = 4 * QUICK + EVEN
    ALONE_AT = SPARSE_AT + 4 * SPARSE
    assert LEAD % 2 == EVEN % 2 == 0 and ALONE_AT <= GROUPS - 5
    W = GROUP * P
    LO_TILES = 2
    HIST_LO, HIST_HI = LO_TILES * P, HI // LO_TILES
    assert HI % LO_TILES == 0 and HIST_HI <= BANK
    assert COPY_ROWS * COPIES == N and E < PARTS * LOW * LOW

    inverse_root_dram = nc.dram_tensor("inverse_root_table", (HI * P, 1), F32, kind="Internal").ap()
    edge_row_dram = nc.dram_tensor("edge_rows", (2, SLOTS * W), F16, kind="Internal").ap()

    with ExitStack() as ctx:
        def sb(name, shape, dt=F32):
            return ctx.enter_context(nc.sbuf_tensor(name, shape, dt))

        def sem(name):
            return ctx.enter_context(nc.semaphore(name))

        table_row = sb("table_row", [HALF, 5, P], F16)
        src_f = sb("src_f", [P, TILES])
        src_i = sb("src_i", [P, TILES], I32)
        dst_i = sb("dst_i", [P, TILES], I32)
        part_i = sb("part_i", [P, 4, TILES], I32)
        lo_f = sb("lo_f", [P, TILES])
        pick_lo = sb("pick_lo", [P, SLOTS * GROUP])
        hi_f = sb("hi_f", [P, TILES])
        src_less_spare = sb("src_less_spare", [P, TILES])
        iota_h = sb("iota_h", [P, HI], F16)
        ident = sb("ident", [P, P])
        later = sb("later", [P, GROUP * P])
        eps = sb("eps", [P, 1])
        chunk_id_i = sb("chunk_id_i", [P, CHUNKS], I32)
        chunk_id = sb("chunk_id", [P, CHUNKS])
        spare_i = sb("spare_i", [P, GROUP], I32)
        spare = sb("spare", [P, GROUP])
        comps_sb = sb("comps_sb", [R, B])
        alpha_sb = sb("alpha_sb", [R, 1])
        scaled_comps = sb("scaled_comps", [R, B])
        comps_rest = sb("comps_rest", [R, B])
        comps_split = sb("comps_split", [R, SPLITS, B], BF16)
        coef = sb("coef", [P, TILES, B])
        work = sb("work", [P, 14 * W + CHUNKS * W + W])

        def part(start, size, dt=F32):
            return work[:, start:start + size].bitcast(dt) if dt != F32 else work[:, start:start + size]

        hot_size = GROUP * HIST_LO
        lo_hot = part(0, hot_size, F16).rearrange("p (b j n) -> p b j n", b=2, j=GROUP)
        hi_hot = part(hot_size, GROUP * HIST_HI, F16).rearrange("p (b j n) -> p b j n", b=2, j=GROUP)
        degree = part(hot_size + GROUP * HIST_HI, HI)
        tables_at = hot_size + GROUP * HIST_HI + HI + CHUNKS * P
        table_i = part(tables_at, 6 * P, I32)[0:HALF, :].rearrange("t (k p) -> t k p", p=P)
        table_f = part(tables_at + 6 * P, 4 * P)[0:HALF, :].rearrange("t (k p) -> t k p", p=P)
        table_hi = part(tables_at + 10 * P, 3 * P, I32)[0:HALF, :].rearrange("t (k p) -> t k p", p=P)
        iota_i = part(tables_at + 13 * P, HI, I32)
        assert tables_at + 13 * P + HI <= 14 * W
        degree_turned = sb("degree_turned", [CH, CHUNKS, P])
        edge_row = sb("edge_row", [P, RING, 2, W], F16)
        node_hot = part(14 * W, CHUNKS * W, F16).rearrange("p (b c e) -> p b c e", b=2, c=CHUNKS)
        type_hot = part((14 + CHUNKS) * W, W, BF16).rearrange("p (b e) -> p b e", b=2)
        degree_i = part(hot_size + GROUP * HIST_HI + HI, CHUNKS * P)[0:CH, :].bitcast(I32).rearrange(
            "p (c l) -> p c l", c=CHUNKS)
        degree_parts = sb("degree_parts", [CH, PARTS, CHUNKS, P], F16)
        inverse_root = sb("inverse_root", [CH, CHUNKS, P])
        masked = sb("masked", [P, GROUP, P])
        gather_idx = sb("gather_idx", [P, 2, GROUP], I32)
        gathered = sb("gathered", [P, 2, GROUP, D])
        rows = sb("rows", [P, TILES, D])
        look_idx = sb("look_idx", [P, 2, GROUP], I32)
        looked = sb("looked", [P, 2, GROUP])
        picked_degree = sb("picked_degree", [P, SLOTS * GROUP])
        picked_norm = sb("picked_norm", [P, SLOTS * GROUP])
        src_norm = sb("src_norm", [P, TILES])
        row_sum = sb("row_sum", [P, 2, GROUP])
        row_squares = sb("row_squares", [P, 2, GROUP])
        mean = sb("mean", [P, 2, GROUP])
        squared = sb("squared", [P, GROUP, D])
        squares = sb("squares", [P, TILES])
        rstd = sb("rstd", [P, TILES])
        shift = sb("shift", [P, TILES])
        bases_sb = sb("bases_sb", [D, B, D])
        h = part(0, 2 * W).rearrange("p (b j d) -> p b j d", b=2, j=GROUP)
        h_turned = part(2 * W, 2 * W).rearrange("p (b j e) -> p b j e", b=2, j=GROUP)
        part_sum = part(4 * W, 2 * W).rearrange("p (b j d) -> p b j d", b=2, j=GROUP)
        src_row = sb("src_row", [P, 2, GROUP * P], I32)
        same = part(6 * W, 8 * W).rearrange("p (b j e) -> p b j e", b=2, j=GROUP)
        copies = sb("copies", [P, 2, GROUP])
        keep = sb("keep", [P, 2, GROUP])
        scatter_idx = sb("scatter_idx", [P, 2, GROUP], I32)
        sums = gathered

        pst = ctx.enter_context(nc.psum_tensor("pst", [P, 8, BANK], F32))

        SUMS, LOOK, TURNED, COEF, PRODUCT = 0, 1, 2, 3, 4

        copied = [sem(f"copied{b}") for b in range(2)]
        spare_filled = sem("spare_filled")
        tables_loaded = sem("tables_loaded")
        padded = sem("padded")
        weights_loaded = sem("weights_loaded")
        iota_ready = sem("iota_ready")
        ident_ready = sem("ident_ready")
        ident_cleared = sem("ident_cleared")
        dve_step = sem("dve_step")
        table_float = sem("table_float")
        table_turned = sem("table_turned")
        idx_ready = sem("idx_ready")
        hot_ready = sem("hot_ready")
        hot_used = sem("hot_used")
        degree_copied = sem("degree_copied")
        degree_turned_ps = sem("degree_turned_ps")
        degree_ready = sem("degree_ready")
        table_clamped = sem("table_clamped")
        table_root = sem("table_root")
        table_ready = sem("table_ready")
        inverse_ready = sem("inverse_ready")
        table_stored = sem("table_stored")
        row_table_ready = sem("row_table_ready")
        rows_stored = sem("rows_stored")
        edge_row_loaded = [sem(f"edge_row_loaded{r}") for r in range(RING)]
        turned_hot_ready = sem("turned_hot_ready")
        look_ps = sem("look_ps")
        picked_ready = sem("picked_ready")
        coef_kept = sem("coef_kept")
        idx_staged = sem("idx_staged")
        row_gathered = [sem(f"row_gathered{b}") for b in range(2)]
        look_staged = sem("look_staged")
        look_done = [sem(f"look_done{b}") for b in range(2)]
        src_norm_ready = sem("src_norm_ready")
        row_summed = sem("row_summed")
        mean_ready = sem("mean_ready")
        row_squared = sem("row_squared")
        squares_kept = sem("squares_kept")
        act_turn = sem("act_turn")
        root_in = sem("root_in")
        root_done = sem("root_done")
        norm_ready = sem("norm_ready")
        h_ready = sem("h_ready")
        h_turned_ps = sem("h_turned_ps")
        h_turned_ready = sem("h_turned_ready")
        product_ready = sem("product_ready")
        first_part = sem("first_part")
        second_part = sem("second_part")
        third_part = sem("third_part")
        message_ready = sem("message_ready")
        src_row_loaded = [sem(f"src_row_loaded{b}") for b in range(2)]
        same_ready = sem("same_ready")
        keep_ready = sem("keep_ready")
        scatter_idx_ready = sem("scatter_idx_ready")
        sums_ps = sem("sums_ps")
        sums_ready = sem("sums_ready")
        scattered = sem("scattered")
        pool_turn = sem("pool_turn")

        def groups(body, eng, first=0, end=GROUPS):
            i = first
            while i < 2:
                body(i, i % 2)
                i += 1
            loop_end = min(end, GROUPS - 3)
            if loop_end > i:
                assert i % 2 == 0 and (loop_end - i) % 2 == 0
                with eng.Fori(i, loop_end - 1, 2) as k:
                    body(k, 0)
                    body(k + 1, 1)
                i = loop_end
            for j in range(i, end):
                body(j, j % 2)

        def slots(body, eng, first, end, own=False):
            assert first % RING == end % RING == 0
            for r in range(RING):
                body(first + r, r, own)
            if end > first + RING:
                with eng.Fori(first + RING, end - RING + 1, RING) as k:
                    for r in range(RING):
                        body(k + r, r, own)

        block = ctx.enter_context(nc.Block())

        @block.sync
        def _(sp):
            def load_table(slot, array):
                sp.dma_start(table_i[:, slot, :], array[0:HALF * P].rearrange("(t p) -> t p", p=P)) \
                    .then_inc(tables_loaded, 16)
                full = (HALF + LAST_ROWS) * P
                sp.dma_start(table_i[0:LAST_ROWS, slot + 1, :],
                             array[HALF * P:full].rearrange("(t p) -> t p", p=P)).then_inc(tables_loaded, 16)
                sp.dma_start(table_i[LAST_ROWS:LAST_ROWS + 1, slot + 1, 0:LAST_EDGES],
                             array[full:E].rearrange("(t p) -> t p", t=1)).then_inc(tables_loaded, 16)

            sp.wait_ge(padded, 4)
            load_table(0, dst)
            load_table(2, src)
            load_table(4, edge_type)
            sp.dma_start(comps_sb[:], comps).then_inc(weights_loaded, 16)
            sp.dma_start(alpha_sb[:], alpha).then_inc(weights_loaded, 16)
            sp.dma_start(bases_sb[:], bases.rearrange("b d f -> d b f")).then_inc(weights_loaded, 16)
            extra = out.shape[0] - N
            sp.dma_start(out[N:N + extra, :], x[0:extra, :]).then_inc(spare_filled, 16)
            sp.wait_ge(row_table_ready, 2)
            for k in range(2):
                sp.dma_start(edge_row_dram[k, OWN * W:SLOTS * W].rearrange("(h t p) -> t h p", h=2, p=P),
                             table_row[:, 3 * k:3 * k + 2, :]).then_inc(rows_stored, 16)
            sp.dma_start(edge_row_dram[0, 0:OWN * W].rearrange("(t p) -> t p", p=P),
                         table_row[0:OWN * GROUP, 2, :]).then_inc(rows_stored, 16)

            def copy(i, b):
                if not (isinstance(i, int) and i < 2):
                    sp.wait_ge(copied[b], (i - b) * 8)
                a = i * COPY_ROWS
                flat_out, flat_x = (y[bass.ds(a, COPY_ROWS), :].rearrange("r d -> (r d)") for y in (out, x))
                sp.dma_start(flat_out.rearrange("(q e) -> q e", q=16), flat_x.rearrange("(q e) -> q e", q=16)) \
                    .then_inc(copied[b], 16)

            copy(0, 0)
            copy(1, 1)
            with sp.Fori(2, EARLY_COPIES - 1, 2) as k:
                copy(k, 0)
                copy(k + 1, 1)
            sp.wait_ge(rows_stored, 48)

            def load_edge_row(i, r, own=False):
                if not (isinstance(i, int) and i < RING):
                    sp.wait_ge(turned_hot_ready, i - RING + 1)
                n = 1 if own else 2
                sp.dma_start(edge_row[:, r, 0:n, :],
                             edge_row_dram[0:n, bass.ds(i * W, W)].rearrange("(o k) e -> o k e", o=1)
                             .to_broadcast([P, n, W])).then_inc(edge_row_loaded[r], 16)

            def load_and_copy(i, r, own):
                load_edge_row(i, r, own)
                for c in range(2):
                    copy(COPIES + 2 * (i - OWN - AHEAD) + c, c)

            slots(load_edge_row, sp, 0, OWN, True)
            slots(load_edge_row, sp, OWN, OWN + AHEAD - LATE)
            slots(load_and_copy, sp, OWN + AHEAD - LATE, OWN + AHEAD, False)

            def load_src_row(i, b):
                last = isinstance(i, int) and i == GROUPS - 1
                if not (isinstance(i, int) and i < 2):
                    sp.wait_ge(same_ready, GROUP * (i - 1))
                n = LAST_GROUP if last else GROUP * P
                sp.dma_start(src_row[:, b, 0:n],
                             src[bass.ds(i * (GROUP * P), n)].rearrange("(o e) -> o e", o=1).to_broadcast([P, n])) \
                    .then_inc(src_row_loaded[b], 16)

            def load_rows(i, r, own):
                load_src_row(i, r % 2)
                load_edge_row(i + OWN + AHEAD, r)

            slots(load_rows, sp, 0, GROUPS - 1 - AHEAD)
            load_rows(GROUPS - 1 - AHEAD, 0, False)
            load_src_row(GROUPS - AHEAD, 1)
            groups(load_src_row, sp, GROUPS - AHEAD + 1, GROUPS)
            sp.wait_ge(spare_filled, 16)
            for b in range(2):
                sp.wait_ge(copied[b], 8 * COPIES)
            sp.wait_ge(rows_stored, 48)
            sp.wait_ge(table_stored, 16)
            sp.wait_ge(scattered, 16 * TILES)

        @block.gpsimd
        def _(pool):
            pool.iota(iota_i[:], [[1, HI]], base=0, channel_multiplier=0).then_inc(iota_ready, 1)
            pool.iota(chunk_id_i[:], [[CH, CHUNKS]], base=0, channel_multiplier=1).then_inc(iota_ready, 1)
            pool.iota(spare_i[:], [[P, GROUP]], base=SPARE, channel_multiplier=1).then_inc(iota_ready, 1)
            pool.memset(ident[:], 0.0).then_inc(ident_cleared, 1)
            pool.memset(later[:], 1.0).then_inc(ident_cleared, 1)
            pool.wait_ge(ident_cleared, 2)
            pool.affine_select(out=ident[:], in_=ident[:], compare_op=ALU.not_equal, fill=1.0, base=0,
                               pattern=[[-1, P]], channel_multiplier=1).then_inc(ident_ready, 1)
            pool.affine_select(out=later[:, 0:P], in_=later[:, 0:P], compare_op=ALU.is_ge, fill=0.0, base=0,
                               pattern=[[1, P]], channel_multiplier=-1).then_inc(ident_ready, 1)

            def gather_rows(i, b):
                if not (isinstance(i, int) and i < 2):
                    pool.wait_ge(row_summed, i - 1)
                pool.wait_ge(idx_staged, i + 1)
                pool.sem_inc(pool_turn)
                for j in range(GROUP):
                    pool.indirect_dma_start(gathered[:, b, j, :], None, x,
                                            bass.IndirectOffsetOnAxis(ap=gather_idx[:, b, j:j + 1], axis=0)) \
                        .then_inc(row_gathered[b], 16)

            groups(gather_rows, pool)

            pool.wait_ge(table_stored, 16)
            pool.wait_ge(idx_ready, 2)

            def keep_looked(i, b):
                pool.wait_ge(look_done[b], (i - b) * (8 * GROUP) + 16 * GROUP)
                pool.tensor_copy(src_norm[:, bass.ds((i + OWN) * GROUP, GROUP)], looked[:, b, :]) \
                    .then_inc(src_norm_ready, 1)

            def stage_look(i, b):
                if not (isinstance(i, int) and i < 2):
                    keep_looked(i - 2, b)
                pool.tensor_copy(look_idx[:, b, :], src_i[:, bass.ds((i + OWN) * GROUP, GROUP)]) \
                    .then_inc(look_staged, 1)
                if not (isinstance(i, int) and i < 2):
                    pool.wait_ge(src_norm_ready, i - 1)
                pool.wait_ge(look_staged, i + 1)
                pool.sem_inc(pool_turn)

            def look_up_tiles(b, tiles):
                for j in tiles:
                    pool.indirect_dma_start(looked[:, b, j:j + 1], None, inverse_root_dram,
                                            bass.IndirectOffsetOnAxis(ap=look_idx[:, b, j:j + 1], axis=0)) \
                        .then_inc(look_done[b], 16)

            def look_up(i, b):
                stage_look(i, b)
                look_up_tiles(b, range(GROUP))

            def scatter(i, b):
                pool.wait_ge(scatter_idx_ready, i + 1)
                pool.wait_ge(sums_ready, GROUP * (i + 1))
                if not (isinstance(i, int) and i == 0):
                    pool.wait_ge(scattered, 16 * GROUP * i)
                pool.sem_inc(pool_turn)
                for j in range(GROUP):
                    pool.indirect_dma_start(out, bass.IndirectOffsetOnAxis(ap=scatter_idx[:, b, j:j + 1], axis=0),
                                            sums[:, b, j, :], None, bounds_check=out.shape[0] - 1,
                                            oob_is_err=True, compute_op=ALU.add).then_inc(scattered, 16)

            groups(look_up, pool, 0, LEAD)
            pool.wait_ge(spare_filled, 16)
            for b in range(2):
                pool.wait_ge(copied[b], 8 * COPIES)

            def four_scatters(k):
                i, n = 4 * k, LEAD + 6 * k
                scatter(i, 0)
                look_up(n, 0)
                look_up(n + 1, 1)
                scatter(i + 1, 1)
                look_up(n + 2, 0)
                scatter(i + 2, 0)
                look_up(n + 3, 1)
                look_up(n + 4, 0)
                scatter(i + 3, 1)
                look_up(n + 5, 1)

            four_scatters(0)
            with pool.Fori(1, QUICK) as k:
                four_scatters(k)

            with pool.Fori(4 * QUICK, SPARSE_AT - 1, 2) as k:
                for b in range(2):
                    scatter(k + b, b)
                    look_up(k + b + LEAD + 2 * QUICK, b)

            with pool.Fori(0, SPARSE) as k:
                for b in range(2):
                    for half in range(2):
                        scatter(SPARSE_AT + 4 * k + 2 * b + half, half)
                        if half == 0:
                            stage_look(SPARSE_AT + LEAD + 2 * QUICK + 2 * k + b, b)
                        look_up_tiles(b, range(half * GROUP // 2, (half + 1) * GROUP // 2))

            scatter(ALONE_AT, 0)
            look_up(GROUPS - OWN - 1, 0)
            scatter(ALONE_AT + 1, 1)
            keep_looked(GROUPS - OWN - 2, 1)
            keep_looked(GROUPS - OWN - 1, 0)
            for i in range(ALONE_AT + 2, GROUPS):
                scatter(i, i % 2)

        @block.vector
        def _(dve):
            steps = [0]

            def step(ins):
                steps[0] += 1
                ins.then_inc(dve_step, 1)
                dve.wait_ge(dve_step, steps[0])

            dve.memset(table_i[:, 1, :], 0).then_inc(padded, 1)
            dve.memset(table_i[:, 3, :], PAD_NODE).then_inc(padded, 1)
            dve.memset(table_i[:, 5, :], 0).then_inc(padded, 1)
            dve.memset(eps[:], EPS).then_inc(padded, 1)
            dve.wait_ge(iota_ready, 3)
            dve.tensor_copy(iota_h[:], iota_i[:])
            dve.tensor_copy(chunk_id[:], chunk_id_i[:])
            step(dve.tensor_copy(spare[:], spare_i[:]))
            dve.wait_ge(tables_loaded, 16 * 9)
            dve.tensor_copy(table_f[:], table_i[:, 0:4, :]).then_inc(table_float, 1)
            step(dve.tensor_scalar(table_hi[:], table_i[:, 0:3, :], P.bit_length() - 1, None,
                                   ALU.logical_shift_right))
            dve.tensor_copy(table_row[:, 0:3, :], table_hi[:]).then_inc(row_table_ready, 1)
            dve.tensor_copy(table_row[:, 3:5, :], table_i[:, 4:6, :]).then_inc(row_table_ready, 1)
            dve.wait_ge(table_turned, 1)
            turned = pst[:, 2, 0:4 * HALF].rearrange("p (k t) -> p k t", k=4)
            dve.tensor_copy(dst_i[:].rearrange("p (k t) -> p k t", k=2), turned[:, 0:2, :]).then_inc(idx_ready, 1)
            dve.wait_ge(idx_ready, 1)
            step(dve.tensor_copy(src_i[:].rearrange("p (k t) -> p k t", k=2), turned[:, 2:4, :]))
            step(dve.tensor_copy(src_f[:].rearrange("p (k t) -> p k t", k=2), turned[:, 2:4, :]))
            step(dve.tensor_scalar(part_i[:, 0, :], src_i[:], HIST_LO.bit_length() - 1, None, ALU.logical_shift_right))
            step(dve.tensor_scalar(part_i[:, 1, :], src_i[:], HIST_LO - 1, None, ALU.bitwise_and))
            step(dve.tensor_scalar(part_i[:, 2, :], dst_i[:], P - 1, None, ALU.bitwise_and))
            step(dve.tensor_scalar(part_i[:, 3, :], src_i[:], P - 1, None, ALU.bitwise_and))
            dve.tensor_copy(hi_f[:], part_i[:, 0, :])
            dve.tensor_copy(pick_lo[:, OWN * GROUP:], part_i[:, 2, :])
            dve.tensor_copy(pick_lo[:, 0:OWN * GROUP], part_i[:, 3, 0:OWN * GROUP])
            step(dve.tensor_copy(lo_f[:], part_i[:, 1, :]))
            step(dve.tensor_tensor(src_less_spare[:].rearrange("p (g j) -> p g j", j=GROUP),
                                   src_f[:].rearrange("p (g j) -> p g j", j=GROUP),
                                   spare[:].rearrange("p (g j) -> p g j", g=1).to_broadcast([P, GROUPS, GROUP]),
                                   ALU.subtract))
            dve.nop().then_inc(idx_ready, 1)

            def hots(i, b):
                if not (isinstance(i, int) and i < 2):
                    dve.wait_ge(hot_used, GROUP * (i - 1))
                for j in range(GROUP):
                    t = i * GROUP + j
                    dve.tensor_scalar(lo_hot[:, b, j, :], iota_h[:, 0:HIST_LO], lo_f[:, bass.ds(t, 1)], None,
                                      ALU.is_equal)
                    dve.tensor_scalar(hi_hot[:, b, j, :], iota_h[:, 0:HIST_HI], hi_f[:, bass.ds(t, 1)], None,
                                      ALU.is_equal).then_inc(hot_ready, 1)

            groups(hots, dve)
            dve.wait_ge(hot_used, TILES)
            for k in range(LO_TILES):
                dve.tensor_copy(degree[:].rearrange("p (h k) -> p k h", k=LO_TILES)[:, k, :], pst[:, k, 0:HIST_HI]) \
                    .then_inc(degree_copied, 1)
            for c in range(CHUNKS):
                dve.wait_ge(degree_turned_ps, min(c - c % 4 + 4, CHUNKS))
                dve.tensor_copy(degree_turned[:, c, :], pst[0:CH, 3 + c // 4, (c % 4) * P:(c % 4 + 1) * P]) \
                    .then_inc(degree_ready, 1)

            dve.wait_ge(degree_ready, CHUNKS)
            dve.tensor_scalar(inverse_root[:], degree_turned[:], 1.0, None, ALU.max).then_inc(table_clamped, 1)
            step(dve.tensor_copy(degree_i[:], degree_turned[:]))
            step(dve.tensor_scalar(degree_i[:], degree_i[:], LOW - 1, None, ALU.bitwise_and))
            step(dve.tensor_copy(degree_parts[:, 0, :, :], degree_i[:]))
            step(dve.tensor_tensor(degree_parts[:, 1, :, :], degree_turned[:], degree_parts[:, 0, :, :],
                                   ALU.subtract))
            dve.wait_ge(weights_loaded, 16 * 3)
            step(dve.tensor_scalar(comps_rest[:], comps_sb[:], alpha_sb[:, 0:1], None, ALU.mult))
            for k in range(SPLITS):
                step(dve.tensor_copy(comps_split[:, k, :], comps_rest[:]))
                if k < SPLITS - 1:
                    step(dve.tensor_tensor(comps_rest[:], comps_rest[:], comps_split[:, k, :], ALU.subtract))
            dve.nop().then_inc(table_ready, 1)

            def turned_hots(i, r, own=False):
                b = r % 2
                dve.wait_ge(edge_row_loaded[r], (i - r) * (16 // RING) + 16)
                if not (isinstance(i, int) and i < 2):
                    dve.wait_ge(look_ps, i - 1)
                for c in range(CHUNKS):
                    last = dve.tensor_scalar(node_hot[0:CH, b, c, :], edge_row[0:CH, r, 0, :],
                                             chunk_id[0:CH, c:c + 1], None, ALU.is_equal)
                if not own:
                    last = dve.tensor_scalar(type_hot[0:R, b, :], edge_row[0:R, r, 1, :], chunk_id[0:R, 0:1], None,
                                             ALU.is_equal)
                last.then_inc(turned_hot_ready, 1)

            def pick(i, bank=0):
                dve.wait_ge(look_ps, i + 1)
                if not (isinstance(i, int) and i < 1):
                    dve.wait_ge(picked_ready, GROUP * i)
                for j in range(GROUP):
                    dve.scalar_tensor_tensor(out=masked[:, j, :], in0=iota_h[:, 0:P],
                                             scalar=pick_lo[:, bass.ds(i * GROUP + j, 1)],
                                             in1=pst[:, LOOK + bank, j * P:(j + 1) * P], op0=ALU.is_equal, op1=ALU.mult,
                                             accum_out=picked_degree[:, bass.ds(i * GROUP + j, 1)]) \
                        .then_inc(picked_ready, 1)

            def keep_coef(i, b, own):
                if not own:
                    dve.tensor_copy(coef[:, bass.ds((i - OWN) * GROUP, GROUP), :].rearrange("p t b -> p (t b)"),
                                    pst[:, COEF + b, 0:GROUP * B]).then_inc(coef_kept, 1)

            def look(i, r, own):
                b = r % 2
                turned_hots(i, r, own)
                if not (isinstance(i, int) and i < 1):
                    pick(i - 1, 1 - b)
                    keep_coef(i - 1, 1 - b, own or (isinstance(i, int) and i == OWN))

            slots(look, dve, 0, OWN, True)
            dve.wait_ge(table_root, 1)
            step(dve.reciprocal(inverse_root[:], inverse_root[:]))
            dve.scalar_tensor_tensor(out=inverse_root[:], in0=degree_turned[:], scalar=1.0, in1=inverse_root[:],
                                     op0=ALU.min, op1=ALU.mult).then_inc(inverse_ready, 1)
            slots(look, dve, OWN, OWN + AHEAD, False)
            pick(OWN + AHEAD - 1, 1)
            keep_coef(OWN + AHEAD - 1, 1, False)

            def norms(first, end, roots):
                t = slice(first * GROUP, end * GROUP)
                n = slice((first + OWN) * GROUP, (end + OWN) * GROUP)
                p = slice(0 if first == 0 else n.start, n.stop)
                dve.wait_ge(picked_ready, GROUP * (end + OWN))
                dve.wait_ge(coef_kept, end)
                dve.tensor_scalar(picked_norm[:, p], picked_degree[:, p], 1.0, None, ALU.max).then_inc(root_in, 1)
                dve.wait_ge(root_done, roots + 1)
                step(dve.reciprocal(rstd[:, t], rstd[:, t]))
                step(dve.tensor_tensor(shift[:, t], shift[:, t], rstd[:, t], ALU.mult))
                dve.wait_ge(root_done, roots + 2)
                step(dve.reciprocal(picked_norm[:, p], picked_norm[:, p]))
                step(dve.scalar_tensor_tensor(out=picked_norm[:, p], in0=picked_degree[:, p], scalar=1.0,
                                              in1=picked_norm[:, p], op0=ALU.min, op1=ALU.mult))
                if first == 0:
                    step(dve.tensor_copy(src_norm[:, 0:OWN * GROUP], picked_norm[:, 0:OWN * GROUP]))
                dve.tensor_tensor(coef[:, t, :], coef[:, t, :],
                                  picked_norm[:, n].rearrange("p (t o) -> p t o", o=1)
                                  .to_broadcast([P, (end - first) * GROUP, B]), ALU.mult).then_inc(norm_ready, 1)

            norms(0, AHEAD, 0)

            def messages(i, b):
                def add(j, term, before, after, out=None):
                    t = i * GROUP + j
                    u = pst[:, PRODUCT + j, term * D:(term + 1) * D]
                    c = coef[:, bass.ds(t, 1), :].rearrange("p a b -> p (a b)")
                    dve.wait_ge(before, t + 1)
                    dve.scalar_tensor_tensor(out=part_sum[:, b, j, :] if out is None else out, in0=u,
                                             scalar=c[:, term:term + 1], in1=part_sum[:, b, j, :],
                                             op0=ALU.mult, op1=ALU.add).then_inc(after, 1)

                for pair in range(0, GROUP, 2):
                    for j in (pair, pair + 1):
                        add(j, 1, first_part, second_part)
                    for j in (pair, pair + 1):
                        add(j, 2, second_part, third_part)
                    for j in (pair, pair + 1):
                        add(j, 3, third_part, message_ready,
                            rows[:, bass.ds(i * GROUP + j, 1), :].rearrange("p a d -> p (a d)"))

            def same_src(i, b):
                if isinstance(i, int) and i == GROUPS - 1:
                    dve.wait_ge(same_ready, GROUP * (GROUPS - 2))
                    dve.memset(src_row[:, b, LAST_GROUP:], PAD_NODE).then_inc(padded, 1)
                    dve.wait_ge(padded, 5)
                dve.wait_ge(src_row_loaded[b], 16 * ((i - b) // 2 + 1) if isinstance(i, int) else
                            (i - b) * 8 + 16)
                if not (isinstance(i, int) and i < 2):
                    dve.wait_ge(sums_ps, i - 1)
                    dve.wait_ge(scattered, 16 * GROUP * (i - 1))
                for j in range(GROUP):
                    t = i * GROUP + j
                    w = (GROUP - j) * P
                    dve.scalar_tensor_tensor(out=same[:, b, j, 0:w], in0=src_row[:, b, j * P:],
                                             scalar=src_f[:, bass.ds(t, 1)], in1=later[:, 0:w],
                                             op0=ALU.is_equal, op1=ALU.mult,
                                             accum_out=copies[:, b, j:j + 1]).then_inc(same_ready, 1)
                dve.wait_ge(same_ready, GROUP * (i + 1))
                dve.scalar_tensor_tensor(out=keep[:, b, :], in0=copies[:, b, :], scalar=1.0,
                                         in1=src_less_spare[:, bass.ds(i * GROUP, GROUP)], op0=ALU.is_equal,
                                         op1=ALU.mult).then_inc(keep_ready, 1)
                dve.wait_ge(keep_ready, i + 1)
                dve.tensor_tensor(scatter_idx[:, b, :], keep[:, b, :], spare[:], ALU.add) \
                    .then_inc(scatter_idx_ready, 1)

            def messages_and_same(i, b):
                messages(i, b)
                same_src(i, b)

            def with_look(i, r, own):
                turned_hots(i + OWN + AHEAD, r)
                messages(i, r % 2)
                same_src(i, r % 2)
                pick(i + OWN + AHEAD)

            slots(with_look, dve, 0, GROUPS - 1 - AHEAD)
            with_look(GROUPS - 1 - AHEAD, 0, False)
            norms(AHEAD, GROUPS, 2)
            messages_and_same(GROUPS - AHEAD, 1)
            groups(messages_and_same, dve, GROUPS - AHEAD + 1, GROUPS)

        @block.scalar
        def _(act):
            def stage_idx(i, b):
                act.activation(gather_idx[:, b, :], dst_i[:, bass.ds(i * GROUP, GROUP)], ACT.Copy) \
                    .then_inc(idx_staged, 1)

            def keep_rows(i, b):
                act.wait_ge(row_gathered[b], (i - b) * (8 * GROUP) + 16 * GROUP)
                if not (isinstance(i, int) and i + 2 >= GROUPS):
                    stage_idx(i + 2, b)
                for j in range(GROUP):
                    last = act.activation(rows[:, bass.ds(i * GROUP + j, 1), :].rearrange("p a d -> p (a d)"),
                                          gathered[:, b, j, :], ACT.Copy, accum_out=row_sum[:, b, j:j + 1])
                last.then_inc(row_summed, 1)
                act.wait_ge(row_summed, i + 1)
                act.activation(mean[:, b, :], row_sum[:, b, :], ACT.Copy, scale=-1.0 / D) \
                    .then_inc(mean_ready, 1)
                act.wait_ge(mean_ready, i + 1)
                act.sem_inc(act_turn)
                for j in range(GROUP):
                    last = act.activation(squared[:, j, :], rows[:, bass.ds(i * GROUP + j, 1), :]
                                          .rearrange("p a d -> p (a d)"), ACT.Square,
                                          bias=mean[:, b, j:j + 1],
                                          accum_out=row_squares[:, b, j:j + 1])
                last.then_inc(row_squared, 1)
                act.wait_ge(row_squared, i + 1)
                act.sem_inc(act_turn)
                act.activation(shift[:, bass.ds(i * GROUP, GROUP)], mean[:, b, :], ACT.Copy)
                act.activation(squares[:, bass.ds(i * GROUP, GROUP)], row_squares[:, b, :], ACT.Copy) \
                    .then_inc(squares_kept, 1)

            act.wait_ge(idx_ready, 1)
            stage_idx(0, 0)
            stage_idx(1, 1)
            groups(keep_rows, act, 0, ROOT_AT)
            act.wait_ge(table_clamped, 1)
            act.activation(inverse_root[:], inverse_root[:], ACT.Sqrt).then_inc(table_root, 1)
            groups(keep_rows, act, ROOT_AT, STORE_AT)
            act.wait_ge(inverse_ready, 1)
            act.dma_start(inverse_root_dram.rearrange("(c r l) o -> r c (l o)", c=CHUNKS, l=P), inverse_root[:]) \
                .then_inc(table_stored, 16)
            groups(keep_rows, act, STORE_AT, GROUPS)

            def roots(first, end, before):
                t = slice(first * GROUP, end * GROUP)
                p = slice(0 if first == 0 else (first + OWN) * GROUP, (end + OWN) * GROUP)
                act.wait_ge(squares_kept, GROUPS)
                act.activation(rstd[:, t], squares[:, t], ACT.Sqrt, bias=eps[:, 0:1], scale=1.0 / D) \
                    .then_inc(root_done, 1)
                act.wait_ge(root_in, before + 1)
                act.activation(picked_norm[:, p], picked_norm[:, p], ACT.Sqrt).then_inc(root_done, 1)

            roots(0, AHEAD, 0)

            def relu(i, b):
                if not (isinstance(i, int) and i < 2):
                    act.wait_ge(h_turned_ps, i - 1)
                for j in range(GROUP):
                    t = i * GROUP + j
                    last = act.activation(h[:, b, j, :], rows[:, bass.ds(t, 1), :].rearrange("p a d -> p (a d)"),
                                          ACT.Relu, bias=shift[:, bass.ds(t, 1)], scale=rstd[:, bass.ds(t, 1)])
                last.then_inc(h_ready, 1)

            def keep_turned(i, b):
                act.wait_ge(h_turned_ps, i + 1)
                if not (isinstance(i, int) and i < 2):
                    act.wait_ge(product_ready, GROUP * (i - 1))
                act.activation(h_turned[:, b, :, :].rearrange("p t e -> p (t e)"), pst[:, TURNED, :], ACT.Copy) \
                    .then_inc(h_turned_ready, 1)

            def first(i, b, j):
                t = i * GROUP + j
                act.wait_ge(product_ready, t + 1)
                if not (isinstance(i, int) and i < 2):
                    act.wait_ge(message_ready, GROUP * (i - 1))
                act.activation(part_sum[:, b, j, :], pst[:, PRODUCT + j, 0:D], ACT.Copy,
                               scale=coef[:, bass.ds(t, 1), :].rearrange("p a b -> p (a b)")[:, 0:1]) \
                    .then_inc(first_part, 1)

            act.wait_ge(norm_ready, 1)
            relu(0, 0)
            relu(1, 1)
            keep_turned(0, 0)

            def transform(i, b):
                first(i, b, 0)
                first(i, b, 1)
                if not (isinstance(i, int) and i + 1 >= GROUPS):
                    keep_turned(i + 1, 1 - b)
                if not (isinstance(i, int) and i + 2 >= GROUPS):
                    relu(i + 2, b)
                first(i, b, 2)
                first(i, b, 3)

            def scale_sums(i, b, own=False):
                act.wait_ge(sums_ps, i + 1)
                if not (own or (isinstance(i, int) and i < OWN)):
                    act.wait_ge(src_norm_ready, i - OWN + 1)
                if not (isinstance(i, int) and i < 2):
                    act.wait_ge(scattered, 16 * GROUP * (i - 1))
                for j in range(GROUP):
                    act.activation(sums[:, b, j, :], pst[:, SUMS, j * P:(j + 1) * P], ACT.Copy,
                                   scale=src_norm[:, bass.ds(i * GROUP + j, 1)]).then_inc(sums_ready, 1)

            def transform_and_scale(i, b, own=False):
                transform(i, b)
                if not (isinstance(i, int) and i < 1):
                    scale_sums(i - 1, 1 - b, own)

            def keep_coef(i):
                act.wait_ge(look_ps, i + 1)
                act.activation(coef[:, bass.ds((i - OWN) * GROUP, GROUP), :].rearrange("p t b -> p (t b)"),
                               pst[:, COEF, 0:GROUP * B], ACT.Copy).then_inc(coef_kept, 1)

            def with_look(i, r, own):
                transform_and_scale(i, r % 2, own)
                keep_coef(i + OWN + AHEAD)

            slots(with_look, act, 0, OWN, True)
            slots(with_look, act, OWN, GROUPS - 1 - AHEAD)
            with_look(GROUPS - 1 - AHEAD, 0, False)
            roots(AHEAD, GROUPS, 1)
            act.wait_ge(norm_ready, 2)
            transform_and_scale(GROUPS - AHEAD, 1)
            groups(transform_and_scale, act, GROUPS - AHEAD + 1, GROUPS)
            scale_sums(GROUPS - 1, 0)

        @block.tensor
        def _(pe):
            pe.wait_ge(ident_ready, 2)
            pe.wait_ge(table_float, 1)
            for k in range(4):
                last = pe.transpose(pst[:, 2, k * HALF:(k + 1) * HALF], table_f[:, k, :], ident[0:HALF, 0:HALF])
            last.then_inc(table_turned, 1)

            def histogram(i, b):
                for j in range(GROUP):
                    t = i * GROUP + j
                    start = isinstance(i, int) and i == 0 and j == 0
                    stop = isinstance(i, int) and i == GROUPS - 1 and j == GROUP - 1
                    pe.wait_ge(hot_ready, t + 1)
                    for k in range(LO_TILES):
                        last = pe.matmul(pst[:, k, 0:HIST_HI], lo_hot[:, b, j, k * P:(k + 1) * P], hi_hot[:, b, j, :],
                                         start=start, stop=stop)
                    last.then_inc(hot_used, 1)

            groups(histogram, pe)
            pe.wait_ge(degree_copied, LO_TILES)
            for c in range(CHUNKS):
                pe.transpose(pst[0:CH, 3 + c // 4, (c % 4) * P:(c % 4 + 1) * P], degree[:, c * CH:(c + 1) * CH],
                             ident[:]).then_inc(degree_turned_ps, 1)

            pe.wait_ge(table_ready, 1)

            def look(i, b, bank, since, own):
                pe.wait_ge(turned_hot_ready, i + 1)
                if not (isinstance(i, int) and i < since):
                    pe.wait_ge(picked_ready, GROUP * (i - since + 1))
                if not own and not (isinstance(i, int) and i < OWN + since):
                    pe.wait_ge(coef_kept, i - OWN - since + 1)
                for j in range(GROUP):
                    for c in range(CHUNKS):
                        for k in range(PARTS):
                            last = pe.matmul(pst[:, LOOK + bank, j * P:(j + 1) * P],
                                             node_hot[0:CH, b, c, j * P:(j + 1) * P], degree_parts[:, k, c, :],
                                             start=(c == 0 and k == 0), stop=(c == CHUNKS - 1 and k == PARTS - 1))
                    if not own:
                        for k in range(SPLITS):
                            last = pe.matmul(pst[:, COEF + bank, j * B:(j + 1) * B], type_hot[0:R, b, j * P:(j + 1) * P],
                                             comps_split[:, k, :], start=(k == 0), stop=(k == SPLITS - 1))
                last.then_inc(look_ps, 1)

            def first_look(i, r, own):
                look(i, r % 2, r % 2, 2, own)

            slots(first_look, pe, 0, OWN, True)
            slots(first_look, pe, OWN, OWN + AHEAD)

            def turn(i, b):
                pe.wait_ge(h_ready, i + 1)
                if not (isinstance(i, int) and i < 1):
                    pe.wait_ge(h_turned_ready, i)
                for j in range(GROUP):
                    last = pe.transpose(pst[:, TURNED, j * P:(j + 1) * P], h[:, b, j, :], ident[:])
                last.then_inc(h_turned_ps, 1)

            def multiply(i, b):
                pe.wait_ge(h_turned_ready, i + 1)
                for j in range(GROUP):
                    if not (isinstance(i, int) and i < 1):
                        pe.wait_ge(message_ready, (i - 1) * GROUP + j + 1)
                    pe.matmul(pst[:, PRODUCT + j, :], h_turned[:, b, j, :], bases_sb[:].rearrange("d b f -> d (b f)"),
                              start=True, stop=True).then_inc(product_ready, 1)

            def add_same(i, b):
                pe.wait_ge(same_ready, GROUP * (i + 1))
                pe.wait_ge(message_ready, GROUP * (i + 1))
                if not (isinstance(i, int) and i < 1):
                    pe.wait_ge(sums_ready, GROUP * i)
                for t in range(GROUP):
                    for s in range(t + 1):
                        last = pe.matmul(pst[:, SUMS, t * P:(t + 1) * P], same[:, b, s, (t - s) * P:(t - s + 1) * P],
                                         rows[:, bass.ds(i * GROUP + s, 1), :].rearrange("p a d -> p (a d)"),
                                         start=(s == 0), stop=(s == t))
                last.then_inc(sums_ps, 1)

            def multiply_and_add(i, b):
                if not (isinstance(i, int) and i + 1 >= GROUPS):
                    turn(i + 1, 1 - b)
                multiply(i, b)
                if not (isinstance(i, int) and i < 1):
                    add_same(i - 1, 1 - b)

            def with_look(i, r, own):
                b = r % 2
                turn(i + 1, 1 - b)
                multiply(i, b)
                if not (isinstance(i, int) and i < 1):
                    add_same(i - 1, 1 - b)
                look(i + OWN + AHEAD, b, 0, 1, False)

            turn(0, 0)
            slots(with_look, pe, 0, GROUPS - 1 - AHEAD)
            with_look(GROUPS - 1 - AHEAD, 0, False)
            multiply_and_add(GROUPS - AHEAD, 1)
            groups(multiply_and_add, pe, GROUPS - AHEAD + 1, GROUPS)
            add_same(GROUPS - 1, 0)


_INS = ['x', 'src', 'dst', 'edge_type_50', 'L0_gnn_bases', 'L0_gnn_comps', 'L0_gnn_alpha']


def kernel(**inputs):
    import numpy as _np
    import concourse.bacc as _bacc
    from concourse import mybir as _mybir
    from concourse.bass_utils import run_bass_kernel_spmd as _run

    nc = _bacc.Bacc("TRN2", target_bir_lowering=False, num_devices=1)
    arrays, args = {}, []
    for name in _INS:
        a = _np.ascontiguousarray(inputs[name])
        arrays[f"in_{name}_dram"] = a
        args.append(nc.dram_tensor(f"in_{name}_dram", a.shape, _mybir.dt.from_np(a.dtype), kind="ExternalInput").ap())
    nodes, width = inputs["x"].shape
    args.append(nc.dram_tensor("out_dram", (padded_rows(nodes), width), _mybir.dt.float32,
                               kind="ExternalOutput").ap())
    build(nc, *args)
    r = _run(nc, [arrays], core_ids=[0])
    return r.results[0]["out_dram"][:nodes]
```
